# Optimizing a Trainium2 kernel written in Bass

```python
import numpy as np
import jax
import jax.numpy as jnp

def _softmax(x, axis=-1):
    return jax.nn.softmax(x, axis=axis)

def _gelu(x):
    return jax.nn.gelu(x, approximate=True)

def _silu(x):
    return jax.nn.silu(x)

def _sigmoid(x):
    return jax.nn.sigmoid(x)

def _layernorm(x, axis=-1, eps=1e-05):
    m = jnp.mean(x, axis=axis, keepdims=True)
    v = jnp.var(x, axis=axis, keepdims=True)
    return (x - m) / jnp.sqrt(v + eps)

def _scatter_add(tgt, idx, src, axis=0):
    return tgt.at[idx].add(src)

def _segment_sum(src, seg, n):
    return jax.ops.segment_sum(src, seg, n)
kernel_name = 'mk_adaln_ffn_d1_seqx_r8_bd1800'

def setup_inputs(seed: int=0):
    np.random.seed(seed)
    _w = jnp.asarray

    def _rec_inputs():
        import jax
        import jax.numpy as jnp
        _rk = jax.random.key(seed)
        x = 7.22e-05 + 1 * jax.random.normal(jax.random.fold_in(_rk, 1), (8, 128, 512), jnp.float32)
        _lenS = 128 - jax.random.randint(jax.random.fold_in(_rk, 7), (8,), 0, max(1, 128 // 4) + 1, jnp.int32)
        _lenS2 = 128 - jax.random.randint(jax.random.fold_in(_rk, 8), (8,), 0, max(1, 128 // 4) + 1, jnp.int32)
        itok_B_2_6 = jax.random.randint(jax.random.fold_in(_rk, 11), (8,), 2, 7, jnp.int32)
        return (x, itok_B_2_6)
    x, itok_B_2_6 = _rec_inputs()

    def _L0_cond_setup():
        import jax, jax.numpy as jnp
        import numpy as np
        B, N, H, F = (4, 64, 512, 1376)
        L, R, RANK = (1, 16, 16)
        SCALE = 0.5
        key = jax.random.key(seed)
        ks = jax.random.split(key, 12)
        nrm = lambda k, shape, fan: jax.random.normal(k, shape, jnp.float32) * fan ** (-0.5)
        inp = {'x': jax.random.normal(ks[0], (B, N, H), jnp.float32), 'W_gate': nrm(ks[1], (F, H), H), 'W_up': nrm(ks[2], (F, H), H), 'W_down': nrm(ks[3], (H, F), F), 'A_gate': nrm(ks[4], (L, R, RANK, H), H), 'B_gate': nrm(ks[5], (L, R, F, RANK), RANK), 'A_up': nrm(ks[6], (L, R, RANK, H), H), 'B_up': nrm(ks[7], (L, R, F, RANK), RANK), 'A_down': nrm(ks[8], (L, R, RANK, F), F), 'B_down': nrm(ks[9], (L, R, H, RANK), RANK), 'lora_indices': jax.random.randint(ks[10], (B,), 0, R), 'layer_idx': 0}
        return inp
    _L0_cond_all = _L0_cond_setup()
    _L0_cond_in = {k: v for k, v in _L0_cond_all.items() if k in ('W_gate', 'W_up', 'W_down', 'A_gate', 'B_gate', 'A_up', 'B_up', 'A_down', 'B_down')}
    del _L0_cond_all

    def _L0_ffn_setup():
        import jax, jax.numpy as jnp
        import numpy as np
        RMS_EPS = 1e-05
        key = jax.random.key(seed)
        k1, k2, k3, k4 = jax.random.split(key, 4)
        B, S, H, I = (1, 256, 512, 1792)
        x = jax.random.normal(k1, (B, S, H), dtype=jnp.float32)
        ln_w = jnp.ones((H,), dtype=jnp.float32)
        gate_w = jax.random.normal(k2, (I, H), dtype=jnp.float32) * 0.02
        up_w = jax.random.normal(k3, (I, H), dtype=jnp.float32) * 0.02
        down_w = jax.random.normal(k4, (H, I), dtype=jnp.float32) * 0.02
        return {'x': x, 'ln_w': ln_w, 'gate_w': gate_w, 'up_w': up_w, 'down_w': down_w}
    _L0_ffn_all = _L0_ffn_setup()
    _L0_ffn_in = {k: v for k, v in _L0_ffn_all.items() if k in ('ln_w', 'gate_w', 'up_w', 'down_w')}
    del _L0_ffn_all
    return {'x': x, 'itok_B_2_6': itok_B_2_6, 'L0_cond_W_gate': _L0_cond_in['W_gate'], 'L0_cond_W_up': _L0_cond_in['W_up'], 'L0_cond_W_down': _L0_cond_in['W_down'], 'L0_cond_A_gate': _L0_cond_in['A_gate'], 'L0_cond_B_gate': _L0_cond_in['B_gate'], 'L0_cond_A_up': _L0_cond_in['A_up'], 'L0_cond_B_up': _L0_cond_in['B_up'], 'L0_cond_A_down': _L0_cond_in['A_down'], 'L0_cond_B_down': _L0_cond_in['B_down'], 'L0_ffn_ln_w': _L0_ffn_in['ln_w'], 'L0_ffn_gate_w': _L0_ffn_in['gate_w'], 'L0_ffn_up_w': _L0_ffn_in['up_w'], 'L0_ffn_down_w': _L0_ffn_in['down_w']}

def reference(x, itok_B_2_6, L0_cond_W_gate, L0_cond_W_up, L0_cond_W_down, L0_cond_A_gate, L0_cond_B_gate, L0_cond_A_up, L0_cond_B_up, L0_cond_A_down, L0_cond_B_down, L0_ffn_ln_w, L0_ffn_gate_w, L0_ffn_up_w, L0_ffn_down_w):
    import jax
    import jax.numpy as jnp

    def _L0_cond_ref(x, W_gate, W_up, W_down, A_gate, B_gate, A_up, B_up, A_down, B_down, lora_indices, layer_idx):
        import jax, jax.numpy as jnp
        import numpy as np
        B, N, H, F = (4, 64, 512, 1376)
        L, R, RANK = (1, 16, 16)
        SCALE = 0.5

        def lora_add(base, inp, A, B):
            Ab = A[layer_idx][lora_indices]
            Bb = B[layer_idx][lora_indices]
            t = jnp.einsum('bri,bni->bnr', Ab, inp)
            return base + jnp.einsum('bor,bnr->bno', Bb, t) * SCALE
        gate = lora_add(jnp.einsum('bnh,fh->bnf', x, W_gate), x, A_gate, B_gate)
        up = lora_add(jnp.einsum('bnh,fh->bnf', x, W_up), x, A_up, B_up)
        act = jax.nn.silu(gate) * up
        down = lora_add(jnp.einsum('bnf,hf->bnh', act, W_down), act, A_down, B_down)
        return down

    def _L0_ffn_ref(x, ln_w, gate_w, up_w, down_w):
        import jax, jax.numpy as jnp
        import numpy as np
        RMS_EPS = 1e-05
        var = jnp.mean(jnp.square(x), axis=-1, keepdims=True)
        nx = x * jax.lax.rsqrt(var + RMS_EPS) * ln_w
        g = jnp.einsum('bsh,ih->bsi', nx, gate_w)
        u = jnp.einsum('bsh,ih->bsi', nx, up_w)
        return jnp.einsum('bsi,hi->bsh', jax.nn.silu(g) * u, down_w)
    x = x + _L0_ffn_ref(_L0_cond_ref(x, L0_cond_W_gate, L0_cond_W_up, L0_cond_W_down, L0_cond_A_gate, L0_cond_B_gate, L0_cond_A_up, L0_cond_B_up, L0_cond_A_down, L0_cond_B_down, itok_B_2_6, 0), L0_ffn_ln_w, L0_ffn_gate_w, L0_ffn_up_w, L0_ffn_down_w)
    return x

_drawn_inputs = setup_inputs


def setup_inputs(seed=0):
    import zlib

    import numpy as np

    out = dict(_drawn_inputs(seed))
    spreads = {'L0_ffn_ln_w': (1.0, 0.534)}
    factors = {}
    for name, (base, spread) in spreads.items():
        noise = np.random.default_rng([zlib.crc32(name.encode()), seed]).standard_normal(out[name].shape)
        drawn = base * np.exp(spread * noise) if base else spread * noise
        out[name] = jnp.asarray(drawn.astype(out[name].dtype))
    for name, factor in factors.items():
        out[name] = (out[name] * factor).astype(out[name].dtype)
    return out
```

```python
from contextlib import ExitStack

import concourse.bass as bass
from concourse import mybir

TOK, H, R, RANK, B = 1024, 512, 16, 16, 8
P = 128
KT = H // P
FC, FF = 11, 14
NT = FC + FF
PAIRS = B // 2
CH = 512
PT = 2 * P
KS = 96
NORM_EPS = 1e-5
LORA_SCALE = 0.5
AD_CUT = 6


def build(nc, xT_in, x_in, idx_in, wgu_in, wd_in, agu_in, bgu_in, ad_in, bd_in, lnw_in, out):
    f32, f32r, i32 = mybir.dt.float32, mybir.dt.float32r, mybir.dt.int32
    ALU, ACT = mybir.AluOpType, mybir.ActivationFunctionType
    ds = bass.ds
    ctx = ExitStack()
    with ctx:
        def sb(name, shape, dt, where=ctx):
            return where.enter_context(nc.sbuf_tensor(name, shape, dt))

        def sem(name):
            return ctx.enter_context(nc.semaphore(name))

        raw_gu = sb("raw_gu", [P, 2, 2, H], f32)
        raw_d = sb("raw_d", [P, 2, H], f32)
        wgu = sb("wgu", [P, 2, 2, 2, H], f32r)
        xT = sb("xT", [P, 2, KT, TOK], f32r)
        wd = sb("wd", [P, FF * 2 * H], f32r)
        pb = sb("pb", [P, FF * 2 * PT], f32r)
        tok = sb("tok", [P, 4, H], f32)
        silu = sb("silu", [P, 2, CH], f32)
        tadd = sb("tadd", [32, 2, PT], f32)
        tsum = sb("tsum", [32, 2, PT], f32)
        mask = sb("mask", [32, 2, PT], f32)
        ident = sb("ident", [P, P], f32)
        lnw = sb("lnw", [P, KT], f32)
        stat = sb("stat", [P, 8], f32)
        idx = sb("idx", [1, B], i32)
        with ExitStack() as early:
            act_c = sb("act_c", [P, FC * TOK], f32, early)
            ad = sb("ad", [P, FC, P], f32r, early)
            ad_raw = sb("ad_raw", [P, B, FC * RANK], f32, early)
        act_f = sb("act_f", [P, FF * TOK], f32)

        wd_t = wd[:, :].rearrange("p (t s h) -> p t s h", t=FF, s=2)
        pb_t = pb[:, :].rearrange("p (t s n) -> p t s n", t=FF, s=2)
        agu = wd[:, 9 * 2 * H:11 * 2 * H].rearrange("p (q k m) -> p q k m", q=PAIRS, k=KT)
        stack = wd[0:KS, 11 * 2 * H:13 * 2 * H].rearrange("p (y q g f) -> p y q g f", y=2, q=PAIRS, g=2)
        bd = wd[0:KS, 11 * 2 * H:13 * 2 * H].rearrange("p (q h) -> p q h", q=PAIRS)
        td = wd[0:KS, 13 * 2 * H:13 * 2 * H + PT]
        bgu = pb[:, 0:4 * FC * P].rearrange("p (s g f) -> p s g f", s=2, g=2)
        tgu01 = wd[0:KS, 13 * 2 * H:14 * 2 * H].rearrange("p (q g n) -> p q g n", q=2, g=2)
        tgu23 = pb[0:KS, 12 * 2 * PT:14 * 2 * PT].rearrange("p (q g n) -> p q g n", q=2, g=2)

        def tgu(q):
            return (tgu01 if q < 2 else tgu23)[:, q % 2]

        ad_hl = ad[:, :, :].rearrange("p t (s b r) -> p t s b r", s=2, b=4)
        agu_raw = act_c[:, 3 * TOK:4 * TOK].rearrange("p (b g k r) -> p b g k r", b=B, g=2, k=KT)
        bgu_raw = act_c[:, 4 * TOK:4 * TOK + 2 * FC * P].rearrange("p (g f) -> p g f", g=2)
        x_raw = act_c[:, 7 * TOK:11 * TOK].rearrange("p (k n) -> p k n", k=KT)
        bd_raw = tok[0:KS, :, :]

        bank = [ctx.enter_context(nc.psum_tensor(f"bank{i}", [P, CH], f32)) for i in range(8)]
        T_BANK = bank[4]
        Y_BANK = [bank[5], bank[2]]
        TR_BANK = [bank[6], bank[7]]
        Z_BANK = [bank[4], bank[5]]

        s_idx = sem("idx_loaded")
        s_lnw = sem("lnw_loaded")
        s_const = sem("consts_made")
        s_memset = sem("memset_done")
        s_x_ld = [[sem(f"x_loaded_{c}{k}") for k in range(KT)] for c in range(2)]
        s_w0_ld = [sem("gate0_loaded"), sem("up0_loaded")]
        s_w_ld = [sem("w_loaded_even"), sem("w_loaded_odd")]
        s_wd_ld = [sem("wd_loaded_even"), sem("wd_loaded_odd")]
        s_agu_ld, s_bgu_ld = sem("agu_loaded"), [sem("bgu_loaded_0"), sem("bgu_loaded_1")]
        s_ad_ld, s_bd_ld = sem("ad_loaded"), sem("bd_loaded")
        s_st_ld = [sem("stack_loaded_even"), sem("stack_loaded_odd")]
        s_hi = {n: sem(f"{n}_hi") for n in ("x", "w", "wd", "agu", "bgu", "ad", "bd", "act", "nx", "t")}
        s_split = {n: sem(f"{n}_split") for n in ("x", "w", "wd", "agu", "bgu", "ad", "bd", "act", "nx")}
        s_gate, s_up = sem("gate_ready"), sem("up_ready")
        s_silu, s_act = sem("silu_done"), sem("act_done")
        s_t, s_tadd, s_tsum, s_tmask, s_tsplit = (sem(n) for n in (
            "t_ready", "tadd_done", "tsum_done", "tmask_done", "t_split"))
        s_pb_used = sem("act_pair_used")
        s_y = sem("y_ready")
        s_ss, s_var, s_std, s_inv = (sem(n) for n in ("squares_done", "var_done", "std_done", "inv_done"))
        s_newton = sem("newton_steps")
        s_y_taken = sem("y_taken")
        s_tr, s_nraw = sem("transposed"), sem("nraw_done")
        s_xr_ld, s_out = [sem("xrow_loaded_0"), sem("xrow_loaded_1")], [sem("out_stored_0"), sem("out_stored_1")]

        block = ctx.enter_context(nc.Block())

        def v32(ap):
            return ap.bitcast(f32)

        def w_loads(i, c):
            return i + (c + 1) // 2

        def wd_loads(i, c):
            return i + c // 2 + 1

        def over_tiles(eng, first, last, body):
            twos = (last - first + 1) // 2
            if twos > 1:
                with eng.Fori(0, twos) as i:
                    body(i, first)
                    body(i, first + 1)
                first += 2 * twos
            for c in range(first, last + 1):
                body(0, c)

        @block.sync
        def _(sp):
            def load_w(i, c):
                n = 2 * i + c
                if not (isinstance(n, int) and n < 2):
                    sp.wait_ge(s_split["w"], 2 * n - 2)
                sp.dma_start(raw_gu[:, c % 2, :, :], wgu_in[ds(n, 1), :, :].rearrange(
                    "o p (g f) -> (o p) g f", g=2)).then_inc(s_w_ld[c % 2], 16)

            def load_wd(i, c):
                n = 2 * i + c
                if not (isinstance(n, int) and n < 1):
                    sp.wait_ge(s_split["wd"], n)
                sp.dma_start(raw_d[:, c % 2, :], wd_in[ds(n, 1), :, :].rearrange(
                    "o p h -> (o p) h")).then_inc(s_wd_ld[c % 2], 16)

            def load_stack(i, c):
                n = 2 * i + c
                for rep, part in enumerate((0, 1, 0)):
                    for q in range(PAIRS):
                        sp.dma_start(v32(stack[32 * rep:32 * rep + 32, c % 2, q]),
                                     v32(bgu[32 * q:32 * q + 32, part, :, ds(n * P, P)])
                                     ).then_inc(s_st_ld[c % 2], 16)

            sp.dma_start(idx[:, :], idx_in[:, :]).then_inc(s_idx, 16)
            sp.dma_start(raw_gu[:, 0, 0, :], wgu_in[0, :, 0:H]).then_inc(s_w0_ld[0], 16)
            for k in range(KT):
                sp.dma_start(x_raw[:, k, 0:CH], xT_in[:, k, 0:CH]).then_inc(s_x_ld[0][k], 16)
            sp.dma_start(raw_gu[:, 0, 1, :], wgu_in[0, :, H:2 * H]).then_inc(s_w0_ld[1], 16)
            sp.dma_start(lnw[:, :], lnw_in[:, :]).then_inc(s_lnw, 16)
            sp.wait_ge(s_idx, 16)
            which = [sp.value_load(idx[0:1, b:b + 1], min_val=0, max_val=R - 1) for b in range(B)]
            for b in range(B):
                sp.dma_start(agu_raw[:, b], agu_in[ds(which[b], 1)].rearrange(
                    "o p (g k r) -> (o p) g k r", g=2, k=KT)).then_inc(s_agu_ld, 16)
            for part, (lo, hi) in enumerate(((0, 2 * P), (2 * P, FC * P))):
                if part == 1:
                    for k in range(KT):
                        sp.dma_start(x_raw[:, k, CH:TOK], xT_in[:, k, CH:TOK]).then_inc(s_x_ld[1][k], 16)
                    load_w(0, 1)
                for b in range(B):
                    sp.dma_start(bgu_raw[RANK * b:RANK * b + RANK, :, lo:hi],
                                 bgu_in[ds(which[b], 1), :, :, lo:hi].rearrange("o r g f -> (o r) g f")
                                 ).then_inc(s_bgu_ld[part], 16)
            sp.wait_ge(s_split["bgu"], 1)
            load_stack(0, 0)
            load_stack(0, 1)
            load_wd(0, 0)
            for b in range(B):
                sp.dma_start(ad_raw[:, b, :], ad_in[ds(which[b], 1)].rearrange("o p f -> (o p) f")
                             ).then_inc(s_ad_ld, 16)
            for rep in range(3):
                for b in range(B):
                    row = 32 * rep + RANK * (b % 2)
                    sp.dma_start(bd_raw[row:row + RANK, b // 2, :],
                                 bd_in[ds(which[b], 1)].rearrange("o r h -> (o r) h")).then_inc(s_bd_ld, 16)
            sp.wait_ge(s_split["bgu"], 2)

            def tile_a(i, c):
                load_w(i, c + 1)
                load_wd(i, c)
                sp.wait_ge(s_up, 4 * i + 2 * c)
                load_stack(i, c + 1)

            over_tiles(sp, 1, FC - 2, tile_a)
            load_w(0, FC)
            load_wd(0, FC - 1)

            def tile_d(i, c):
                load_w(i, c + 1)
                load_wd(i, c)

            over_tiles(sp, FC, NT - 2, tile_d)
            load_wd(0, NT - 1)

            for t in range(2):
                sp.wait_ge(s_y_taken, 8)
                sp.dma_start(tok[:, 2 + t, :], x_in[t * P:t * P + P, :]).then_inc(s_xr_ld[t], 16)

            def store(q, t):
                sp.wait_ge(s_y_taken, 2 * q + t + 9)
                sp.dma_start(out[ds(q * PT + t * P, P), :], tok[:, 2 + t, :]).then_inc(s_out[t], 16)

            with sp.Fori(0, PAIRS - 1) as q:
                for t in range(2):
                    store(q, t)
                    sp.wait_ge(s_out[t], 16 * q + 16)
                    sp.dma_start(tok[:, 2 + t, :], x_in[ds(q * PT + PT + t * P, P), :]).then_inc(s_xr_ld[t], 16)
            for t in range(2):
                store(PAIRS - 1, t)
            for t in range(2):
                sp.wait_ge(s_out[t], 16 * PAIRS)

        @block.gpsimd
        def _(pool):
            nc.gpsimd.memset(ident[:, :], 0.0).then_inc(s_memset, 1)
            nc.gpsimd.memset(mask[:, :, :], LORA_SCALE).then_inc(s_memset, 1)
            nc.gpsimd.memset(v32(ad[:, :, :]), 0.0).then_inc(s_const, 1)
            pool.wait_ge(s_memset, 2)
            nc.gpsimd.affine_select(out=ident[:, :], in_=ident[:, :], compare_op=ALU.not_equal, fill=1.0,
                                    base=0, pattern=[[-1, P]], channel_multiplier=1).then_inc(s_const, 1)
            nc.gpsimd.affine_select(out=mask[:, :, 0:P], in_=mask[:, :, 0:P], compare_op=ALU.is_ge, fill=0.0,
                                    base=RANK - 1, pattern=[[0, 2], [0, P]], channel_multiplier=-1
                                    ).then_inc(s_const, 1)
            nc.gpsimd.affine_select(out=mask[:, :, P:PT], in_=mask[:, :, P:PT], compare_op=ALU.is_ge, fill=0.0,
                                    base=-RANK, pattern=[[0, 2], [0, P]], channel_multiplier=1
                                    ).then_inc(s_const, 1)

        @block.scalar
        def _(a):
            def hi(name, out, raw):
                nc.scalar.activation(out, raw, ACT.Copy).then_inc(s_hi[name], 1)

            def hi_x(c):
                for k in range(KT):
                    a.wait_ge(s_x_ld[c][k], 16)
                    hi("x", xT[:, 0, k, c * CH:(c + 1) * CH], x_raw[:, k, c * CH:(c + 1) * CH])

            def hi_w(i, c):
                a.wait_ge(s_w_ld[c % 2], 16 * w_loads(i, c))
                if not (isinstance(i, int) and c < 2):
                    a.wait_ge(s_up, 4 * i + 2 * c - 2)
                for g in range(2):
                    hi("w", wgu[:, c % 2, g, 0, :], raw_gu[:, c % 2, g, :])

            def hi_wd(i, c, base):
                a.wait_ge(s_wd_ld[c % 2], 16 * wd_loads(i, c))
                hi("wd", wd[:, ds((2 * i + c - base) * 2 * H, H)], raw_d[:, c % 2, :])

            def do_silu(i, c, chunk):
                n = 2 * i + c
                a.wait_ge(s_gate, 2 * n + chunk + 1)
                if not (isinstance(n, int) and n < 1):
                    a.wait_ge(s_act, 2 * n - 2 + chunk + 1)
                nc.scalar.activation(silu[:, chunk, :], bank[2 * chunk][:, :], ACT.Silu).then_inc(s_silu, 1)

            def t_parts(m, banks):
                a.wait_ge(s_t, m + 1)
                for j, (src, row) in enumerate(banks):
                    ins = nc.scalar.activation(tadd[:, j, :], src[row:row + 32, 0:PT], ACT.Copy)
                ins.then_inc(s_tadd, 1)

            def act_pair(q, tiles, act, before):
                for ft in tiles:
                    if before is not None and ft == FF - 1:
                        a.wait_ge(s_y, 2 * q + 8)
                    elif before is not None:
                        a.wait_ge(s_pb_used, before + ft + 1)
                    hi("act", pb_t[:, ft, 0, :], act[:, ds(q * PT + ft * TOK, PT)])

            def ad_pair(q, lo, n):
                for b in range(2):
                    ins = nc.scalar.activation(
                        ad_hl[:, lo:lo + n, 0, b, :],
                        ad_raw[:, ds(2 * q + b, 1), lo * RANK:(lo + n) * RANK].rearrange(
                            "p o (t r) -> p (o t) r", r=RANK), ACT.Copy)
                ins.then_inc(s_hi["ad"], 1)

            a.wait_ge(s_w0_ld[0], 16)
            hi("w", wgu[:, 0, 0, 0, :], raw_gu[:, 0, 0, :])
            hi_x(0)
            a.wait_ge(s_w0_ld[1], 16)
            hi("w", wgu[:, 0, 1, 0, :], raw_gu[:, 0, 1, :])
            a.wait_ge(s_agu_ld, 16 * B)
            agu_out = agu.rearrange("p q k (s g b r) -> p q k s g b r", s=2, g=2, b=2)
            agu_in4 = agu_raw.rearrange("p (q b) g k r -> p q b g k r", b=2)
            for g in range(2):
                for b in range(2):
                    hi("agu", agu_out[:, :, :, 0, g, b, :], agu_in4[:, :, b, g, :, :])
            a.wait_ge(s_bgu_ld[0], 16 * B)
            hi("bgu", bgu[:, 0, :, 0:2 * P], bgu_raw[:, :, 0:2 * P])
            hi_x(1)

            def t_gate_up(q):
                t_parts(q, [(bank[4 + q], 64), (bank[4 + q], 96)])
                a.wait_ge(s_tmask, q + 1)
                nc.scalar.activation(tgu(q)[0:32], tsum[:, :, :], ACT.Copy).then_inc(s_hi["t"], 1)

            t_gate_up(0)
            t_gate_up(1)
            hi_w(0, 1)
            a.wait_ge(s_bgu_ld[1], 16 * B)
            hi("bgu", bgu[:, 0, :, 2 * P:FC * P], bgu_raw[:, :, 2 * P:FC * P])
            t_gate_up(2)
            t_gate_up(3)
            hi_wd(0, 0, 0)
            do_silu(0, 0, 0)
            do_silu(0, 0, 1)

            def tile(i, c, base):
                hi_w(i, c + 1)
                hi_wd(i, c, base)
                do_silu(i, c, 0)
                do_silu(i, c, 1)

            over_tiles(a, 1, FC - 2, lambda i, c: tile(i, c, 0))
            hi_w(0, FC)
            hi_wd(0, FC - 1, 0)
            do_silu(0, FC - 1, 0)
            for y in range(2):
                a.wait_ge(s_st_ld[y], 16 * 12 * (FC // 2 + 1 - y))
            a.wait_ge(s_ad_ld, 16 * B)
            a.wait_ge(s_const, 4)
            ad_pair(0, 0, AD_CUT)
            ad_pair(0, AD_CUT, FC - AD_CUT)
            a.wait_ge(s_act, 2 * FC - 1)
            act_pair(0, range(FC), act_c, None)
            do_silu(0, FC - 1, 1)
            a.wait_ge(s_bd_ld, 16 * 3 * B)
            a.wait_ge(s_up, 2 * FC)
            hi("bd", bd, bd_raw)

            def norm(q, t):
                m = 2 * q + t
                a.wait_ge(s_y, m + 1)
                nc.scalar.activation(silu[:, 0, :], Y_BANK[t][:, :], ACT.Square,
                                     accum_out=stat[:, 0:1]).then_inc(s_ss, 1)
                a.wait_ge(s_var, m + 1)
                nc.scalar.activation(stat[:, 2:3], stat[:, 1:2], ACT.Sqrt).then_inc(s_std, 1)

            def hi_nx(q, t):
                m = 2 * q + t
                a.wait_ge(s_nraw, m + 1)
                hi("nx", xT[:, 0, :, ds(m * P, P)], silu[:, 1, :].rearrange("p (k n) -> p k n", k=KT))

            def pair_b(q, last):
                t_parts(PAIRS + q, [(T_BANK, 64)])
                a.wait_ge(s_tmask, PAIRS + q + 1)
                nc.scalar.activation(td[0:32], tsum[:, 0, :], ACT.Copy).then_inc(s_hi["t"], 1)
                if not last:
                    act_pair(q + 1, range(0, AD_CUT), act_c, q * FC)
                    ad_pair(q + 1, 0, AD_CUT)
                norm(q, 0)
                if not last:
                    act_pair(q + 1, range(AD_CUT, FC), act_c, q * FC)
                    ad_pair(q + 1, AD_CUT, FC - AD_CUT)
                hi_nx(q, 0)
                norm(q, 1)
                hi_nx(q, 1)

            with a.Fori(0, PAIRS - 1) as q:
                pair_b(q, False)
            pair_b(PAIRS - 1, True)

            over_tiles(a, FC, NT - 2, lambda i, c: tile(i, c, FC))
            hi_wd(0, NT - 1, FC)
            do_silu(0, NT - 1, 0)
            a.wait_ge(s_act, 2 * NT - 1)
            act_pair(0, range(FF), act_f, None)
            do_silu(0, NT - 1, 1)
            a.wait_ge(s_act, 2 * NT)
            with a.Fori(1, PAIRS) as q:
                act_pair(q, range(FF), act_f, PAIRS * FC + (q - 1) * (FF - 1))

        @block.vector
        def _(v):
            def sub(out, raw, part):
                return nc.vector.tensor_tensor(out, raw, v32(part), ALU.subtract)

            def lo(name, count, out, raw, part):
                v.wait_ge(s_hi[name], count)
                sub(out, raw, part).then_inc(s_split[name], 1)

            def lo_x(c):
                for k in range(KT):
                    cols = slice(c * CH, (c + 1) * CH)
                    lo("x", KT * c + k + 1, xT[:, 1, k, cols], x_raw[:, k, cols], xT[:, 0, k, cols])

            def lo_w(i, c, g):
                lo("w", 4 * i + 2 * c + g + 1, wgu[:, c % 2, g, 1, :], raw_gu[:, c % 2, g, :],
                   wgu[:, c % 2, g, 0, :])

            def lo_wd(i, c, base):
                n = 2 * i + c
                at = (n - base) * 2 * H
                lo("wd", n + 1, wd[:, ds(at + H, H)], raw_d[:, c % 2, :], wd[:, ds(at, H)])

            def do_act(i, c, chunk, act, base):
                n = 2 * i + c
                v.wait_ge(s_up, 2 * n + chunk + 1)
                v.wait_ge(s_silu, 2 * n + chunk + 1)
                nc.vector.tensor_tensor(act[:, ds((n - base) * TOK + chunk * CH, CH)], silu[:, chunk, :],
                                        bank[2 * chunk + 1][:, :], ALU.mult).then_inc(s_act, 1)

            def t_whole(m, banks, out):
                k = len(banks)
                v.wait_ge(s_tadd, m + 1)
                if not (isinstance(m, int) and m < 1):
                    v.wait_ge(s_tsplit, m)
                for j, (src, row) in enumerate(banks):
                    ins = nc.vector.tensor_tensor(tsum[:, j, :], src[row:row + 32, 0:PT], tadd[:, j, :], ALU.add)
                ins.then_inc(s_tsum, 1)
                v.wait_ge(s_tsum, m + 1)
                nc.vector.tensor_tensor(tsum[:, 0:k, :], tsum[:, 0:k, :], mask[:, 0:k, :], ALU.mult
                                        ).then_inc(s_tmask, 1)
                v.wait_ge(s_hi["t"], m + 1)
                whole = tsum[:, :, :] if k == 2 else tsum[:, 0, :]
                nc.vector.tensor_copy(out[32:64], v32(out[0:32]))
                sub(out[64:96], whole, out[0:32]).then_inc(s_tsplit, 1)

            def act_pair(q, tiles, act, count):
                for ft in tiles:
                    lo("act", count + ft + 1, pb_t[:, ft, 1, :], act[:, ds(q * PT + ft * TOK, PT)],
                       pb_t[:, ft, 0, :])

            def ad_pair(q, lo_t, n, count):
                v.wait_ge(s_hi["ad"], count)
                for b in range(2):
                    ins = sub(ad_hl[:, lo_t:lo_t + n, 1, b, :],
                              ad_raw[:, ds(2 * q + b, 1), lo_t * RANK:(lo_t + n) * RANK].rearrange(
                                  "p o (t r) -> p (o t) r", r=RANK), ad_hl[:, lo_t:lo_t + n, 0, b, :])
                ins.then_inc(s_split["ad"], 1)

            lo_w(0, 0, 0)
            lo_x(0)
            lo_w(0, 0, 1)
            agu_out = agu.rearrange("p q k (s g b r) -> p q k s g b r", s=2, g=2, b=2)
            agu_in4 = agu_raw.rearrange("p (q b) g k r -> p q b g k r", b=2)
            for g in range(2):
                for b in range(2):
                    lo("agu", 2 * g + b + 1, agu_out[:, :, :, 1, g, b, :], agu_in4[:, :, b, g, :, :],
                       agu_out[:, :, :, 0, g, b, :])
            lo("bgu", 1, bgu[:, 1, :, 0:2 * P], bgu_raw[:, :, 0:2 * P], bgu[:, 0, :, 0:2 * P])
            lo_x(1)
            v.wait_ge(s_const, 4)

            def t_gate_up(q):
                t_whole(q, [(bank[4 + q], 0), (bank[4 + q], 32)], tgu(q))

            t_gate_up(0)
            t_gate_up(1)
            lo_w(0, 1, 0)
            lo_w(0, 1, 1)
            lo("bgu", 2, bgu[:, 1, :, 2 * P:FC * P], bgu_raw[:, :, 2 * P:FC * P], bgu[:, 0, :, 2 * P:FC * P])
            t_gate_up(2)
            t_gate_up(3)
            lo_wd(0, 0, 0)
            do_act(0, 0, 0, act_c, 0)
            do_act(0, 0, 1, act_c, 0)

            def tile(i, c, act, base):
                lo_w(i, c + 1, 0)
                lo_w(i, c + 1, 1)
                lo_wd(i, c, base)
                do_act(i, c, 0, act, base)
                do_act(i, c, 1, act, base)

            over_tiles(v, 1, FC - 2, lambda i, c: tile(i, c, act_c, 0))
            lo_w(0, FC, 0)
            lo_w(0, FC, 1)
            lo_wd(0, FC - 1, 0)
            do_act(0, FC - 1, 0, act_c, 0)
            ad_pair(0, 0, AD_CUT, 1)
            ad_pair(0, AD_CUT, FC - AD_CUT, 2)
            act_pair(0, range(FC), act_c, 0)
            do_act(0, FC - 1, 1, act_c, 0)
            lo("bd", 1, bd[32:64], bd_raw[32:64], bd[32:64])
            v.wait_ge(s_lnw, 16)

            def norm(q, t):
                m = 2 * q + t
                v.wait_ge(s_ss, m + 1)
                nc.vector.tensor_scalar(stat[:, 1:2], stat[:, 0:1], 1.0 / H, NORM_EPS, ALU.mult, ALU.add
                                        ).then_inc(s_var, 1)
                v.wait_ge(s_std, m + 1)
                nc.vector.reciprocal(stat[:, 3:4], stat[:, 2:3]).then_inc(s_inv, 1)
                v.wait_ge(s_inv, m + 1)
                steps = [
                    lambda: nc.vector.tensor_scalar(stat[:, 4:5], stat[:, 3:4], stat[:, 3:4], stat[:, 1:2],
                                                    ALU.mult, ALU.mult),
                    lambda: nc.vector.tensor_scalar(stat[:, 5:6], stat[:, 4:5], -0.5, 1.5, ALU.mult, ALU.add),
                    lambda: nc.vector.tensor_tensor(stat[:, 6:7], stat[:, 3:4], stat[:, 5:6], ALU.mult),
                ]
                for k, step in enumerate(steps):
                    step().then_inc(s_newton, 1)
                    v.wait_ge(s_newton, 3 * m + k + 1)
                nc.vector.tensor_scalar(tok[:, t, :], Y_BANK[t][:, :], stat[:, 6:7], None, ALU.mult
                                        ).then_inc(s_y_taken, 1)

            def lo_nx(q, t):
                m = 2 * q + t
                raw = silu[:, 1, :].rearrange("p (k n) -> p k n", k=KT)
                v.wait_ge(s_tr, m + 1)
                nc.vector.tensor_tensor(raw, TR_BANK[t][:, :].rearrange("p (k n) -> p k n", k=KT),
                                        lnw[:, :].unsqueeze(2).to_broadcast([P, KT, P]), ALU.mult
                                        ).then_inc(s_nraw, 1)
                lo("nx", m + 1, xT[:, 1, :, ds(m * P, P)], raw, xT[:, 0, :, ds(m * P, P)])

            def pair_b(q, last):
                t_whole(PAIRS + q, [(T_BANK, 0)], td)
                if not last:
                    act_pair(q + 1, range(0, AD_CUT), act_c, (q + 1) * FC)
                    ad_pair(q + 1, 0, AD_CUT, 2 * q + 3)
                norm(q, 0)
                if not last:
                    act_pair(q + 1, range(AD_CUT, FC), act_c, (q + 1) * FC)
                    ad_pair(q + 1, AD_CUT, FC - AD_CUT, 2 * q + 4)
                lo_nx(q, 0)
                norm(q, 1)
                lo_nx(q, 1)

            with v.Fori(0, PAIRS - 1) as q:
                pair_b(q, False)
            pair_b(PAIRS - 1, True)

            over_tiles(v, FC, NT - 2, lambda i, c: tile(i, c, act_f, FC))
            lo_wd(0, NT - 1, FC)
            do_act(0, NT - 1, 0, act_f, FC)
            act_pair(0, range(FF), act_f, PAIRS * FC)
            do_act(0, NT - 1, 1, act_f, FC)

            def add_x(q, t):
                v.wait_ge(s_xr_ld[t], 16 * q + 16)
                v.wait_ge(s_y, 2 * q + t + 9)
                nc.vector.tensor_tensor(tok[:, 2 + t, :], tok[:, 2 + t, :], Z_BANK[t][:, :], ALU.add
                                        ).then_inc(s_y_taken, 1)

            with v.Fori(0, PAIRS - 1) as q:
                add_x(q, 0)
                act_pair(q + 1, range(FF), act_f, PAIRS * FC + (q + 1) * FF)
                add_x(q, 1)
            add_x(PAIRS - 1, 0)
            add_x(PAIRS - 1, 1)

        @block.tensor
        def _(pe):
            mm = nc.tensor.matmul
            PASSES = ((0, 0), (0, 1), (1, 0))

            def project(par, g, chunk, lora, first=None):
                for k in range(KT):
                    if first is not None:
                        pe.wait_ge(s_split["x"], first + k)
                    for s, r in PASSES:
                        last = k == KT - 1 and s == 1 and not lora
                        ins = mm(bank[2 * chunk + g][:, :], wgu[:, par, g, s, k * P:(k + 1) * P],
                                 xT[:, r, k, chunk * CH:(chunk + 1) * CH],
                                 start=(k == 0 and s == 0 and r == 0), stop=last)
                return ins

            def lora_gu(par, g, chunk):
                for q in (2 * chunk, 2 * chunk + 1):
                    half = (q % 2) * PT
                    ins = mm(bank[2 * chunk + g][:, half:half + PT], stack[:, par, q, g, :], tgu(q)[:, g, :],
                             start=False, stop=(q % 2 == 1))
                ins.then_inc((s_gate, s_up)[g], 1)
                return ins

            def t_gate_up(q):
                for k in range(KT):
                    for r in range(2):
                        ins = mm(bank[4 + q][:, 0:PT], agu[:, q, k, :], xT[:, r, k, q * PT:(q + 1) * PT],
                                 start=(k == 0 and r == 0), stop=(k == KT - 1 and r == 1))
                ins.then_inc(s_t, 1)

            pe.wait_ge(s_split["w"], 1)
            project(0, 0, 0, True, first=1)
            pe.wait_ge(s_split["w"], 2)
            project(0, 1, 0, True)
            pe.wait_ge(s_split["agu"], 4)
            t_gate_up(0)
            t_gate_up(1)
            project(0, 0, 1, True, first=KT + 1)
            t_gate_up(2)
            t_gate_up(3)
            pe.wait_ge(s_st_ld[0], 16 * 12)
            pe.wait_ge(s_tsplit, 2)
            lora_gu(0, 0, 0)
            lora_gu(0, 1, 0)
            project(0, 1, 1, True)
            pe.wait_ge(s_tsplit, 4)
            lora_gu(0, 0, 1)
            lora_gu(0, 1, 1)

            def tile(i, c, lora, between=None):
                n = 2 * i + c
                for chunk in range(2):
                    for g in range(2):
                        if chunk == 0:
                            pe.wait_ge(s_split["w"], 2 * n + g + 1)
                            if lora and g == 0:
                                pe.wait_ge(s_st_ld[c % 2], 16 * 12 * wd_loads(i, c))
                        pe.wait_ge((s_silu, s_act)[g], 2 * n - 2 + chunk + 1)
                        ins = project(c % 2, g, chunk, lora)
                        if lora:
                            ins = lora_gu(c % 2, g, chunk)
                        else:
                            ins.then_inc((s_gate, s_up)[g], 1)
                    if between and chunk == 0:
                        between()
                return ins

            over_tiles(pe, 1, FC - 1, lambda i, c: tile(i, c, True))

            def down(bank_y, ft, t):
                for s, r in ((0, 0), (0, 1), (1, 0)):
                    ins = mm(bank_y[:, :], pb_t[:, ft, s, t * P:(t + 1) * P], wd_t[:, ft, r, :],
                             start=(ft == 0 and s == 0 and r == 0), stop=False)
                return ins

            def lora_down(q, t):
                mm(Y_BANK[t][:, :], td[:, t * P:(t + 1) * P], bd[:, ds(q, 1), :].rearrange("p o h -> p (o h)"),
                   start=False, stop=True).then_inc(s_y, 1)

            def transposes(q, t):
                pe.wait_ge(s_y_taken, 2 * q + t + 1)
                for k in range(KT):
                    ins = nc.tensor.transpose(TR_BANK[t][:, k * P:(k + 1) * P], tok[:, t, k * P:(k + 1) * P],
                                              ident[:, :])
                ins.then_inc(s_tr, 1)

            def pair_b(q, first):
                if not first:
                    pe.wait_ge(s_y_taken, 2 * q - 1)
                for ft in range(FC):
                    pe.wait_ge(s_split["act"], q * FC + ft + 1)
                    if ft in (0, AD_CUT):
                        pe.wait_ge(s_split["ad"], 2 * q + 1 + (ft > 0))
                    for r in range(2):
                        ins = mm(T_BANK[:, 0:PT], ad[:, ft, :], pb_t[:, ft, r, :],
                                 start=(ft == 0 and r == 0), stop=(ft == FC - 1 and r == 1))
                    if ft == FC - 1:
                        ins.then_inc(s_t, 1)
                    down(Y_BANK[0], ft, 0)
                    if ft == 5 and not first:
                        transposes(q - 1, 1)
                if first:
                    pe.wait_ge(s_silu, 2 * FC)
                for ft in range(FC):
                    down(Y_BANK[1], ft, 1).then_inc(s_pb_used, 1)
                    if ft == 4:
                        if first:
                            pe.wait_ge(s_split["bd"], 1)
                        pe.wait_ge(s_tsplit, PAIRS + q + 1)
                        lora_down(q, 0)
                transposes(q, 0)
                lora_down(q, 1)

            pe.wait_ge(s_split["wd"], FC)
            pe.wait_ge(s_const, 4)
            pair_b(0, True)
            with pe.Fori(1, PAIRS) as q:
                pair_b(q, False)

            def second_half():
                transposes(PAIRS - 1, 1)
                pe.wait_ge(s_split["nx"], 8)

            pe.wait_ge(s_split["nx"], 4)
            tile(0, FC, False, second_half)
            over_tiles(pe, FC + 1, NT - 1, lambda i, c: tile(i, c, False))

            pe.wait_ge(s_split["wd"], NT)
            with pe.Fori(0, PAIRS) as q:
                for t in range(2):
                    pe.wait_ge(s_y_taken, 2 * q + t + 7)
                    for ft in range(FF):
                        if t == 0:
                            pe.wait_ge(s_split["act"], PAIRS * FC + q * FF + ft + 1)
                        for s, r in PASSES:
                            ins = mm(Z_BANK[t][:, :], pb_t[:, ft, s, t * P:(t + 1) * P], wd_t[:, ft, r, :],
                                     start=(ft == 0 and s == 0 and r == 0), stop=(ft == FF - 1 and s == 1))
                        if ft == FF - 1:
                            ins.then_inc(s_y, 1)
                        elif t == 1:
                            ins.then_inc(s_pb_used, 1)


def kernel(**inputs):
    import numpy as np
    import concourse.bacc as bacc
    from concourse.bass_utils import run_bass_kernel_spmd

    def arr(name):
        return np.asarray(inputs[name])

    def pad_rows(w, rows):
        return np.concatenate([w, np.zeros((rows - w.shape[0],) + w.shape[1:], w.dtype)], 0)

    def gate_up(gate, up, tiles):
        both = np.stack([pad_rows(gate, tiles * P), pad_rows(up, tiles * P)])
        return both.reshape(2, tiles, P, KT, P).transpose(1, 4, 0, 3, 2).reshape(tiles, P, 2 * H)

    def down(w, tiles):
        return pad_rows(w.T, tiles * P).reshape(tiles, P, H)

    x = arr("x").reshape(TOK, H)
    a_gu = np.stack([arr("L0_cond_A_gate")[0], arr("L0_cond_A_up")[0]])
    b_gu = np.stack([arr("L0_cond_B_gate")[0], arr("L0_cond_B_up")[0]])
    b_gu = np.concatenate([b_gu, np.zeros((2, R, FC * P - b_gu.shape[2], RANK), b_gu.dtype)], 2)
    a_d = arr("L0_cond_A_down")[0]
    a_d = np.concatenate([a_d, np.zeros((R, RANK, FC * P - a_d.shape[2]), a_d.dtype)], 2)
    feeds = {
        "xT_in": x.T.reshape(KT, P, TOK).transpose(1, 0, 2),
        "x_in": x,
        "idx_in": arr("itok_B_2_6").reshape(1, B),
        "wgu_in": np.concatenate([gate_up(arr("L0_cond_W_gate"), arr("L0_cond_W_up"), FC),
                                  gate_up(arr("L0_ffn_gate_w"), arr("L0_ffn_up_w"), FF)], 0),
        "wd_in": np.concatenate([down(arr("L0_cond_W_down"), FC), down(arr("L0_ffn_down_w"), FF)], 0),
        "agu_in": a_gu.reshape(2, R, RANK, KT, P).transpose(1, 4, 0, 3, 2).reshape(R, P, 2 * KT * RANK),
        "bgu_in": b_gu.transpose(1, 3, 0, 2),
        "ad_in": a_d.reshape(R, RANK, FC, P).transpose(0, 3, 2, 1).reshape(R, P, FC * RANK),
        "bd_in": arr("L0_cond_B_down")[0].transpose(0, 2, 1),
        "lnw_in": arr("L0_ffn_ln_w").reshape(KT, P).T,
    }
    feeds = {k: np.ascontiguousarray(v) for k, v in feeds.items()}
    nc = bacc.Bacc("TRN2", target_bir_lowering=False, num_devices=1, dynamic_dma_scratch_size=1024)
    args = [nc.dram_tensor(k, v.shape, mybir.dt.from_np(v.dtype), kind="ExternalInput").ap()
            for k, v in feeds.items()]
    out = nc.dram_tensor("out", (TOK, H), mybir.dt.float32, kind="ExternalOutput").ap()
    build(nc, *args, out)
    r = run_bass_kernel_spmd(nc, [feeds], core_ids=[0])
    return r.results[0]["out"].reshape(B, P, H)
```

```python
from contextlib import ExitStack

import concourse.bass as bass
from concourse import mybir

TOK, H, R, RANK, B = 1024, 512, 16, 16, 8
P = 128
KT = H // P
FC, FF = 11, 14
NT = FC + FF
PAIRS = B // 2
CH = 512
PT = 2 * P
KS = 96
CR = 1376 - (FC - 1) * P
NORM_EPS = 1e-5
LORA_SCALE = 0.5
WARM = 12
B_CUT = 2 * 2 * P


def build(nc, xT_in, x_in, idx_in, wgu_in, wd_in, agu_in, bgu_in, ad_in, bd_in, lnw_in, out):
    f32, f32r, i32 = mybir.dt.float32, mybir.dt.float32r, mybir.dt.int32
    ALU, ACT = mybir.AluOpType, mybir.ActivationFunctionType
    ds = bass.ds
    ctx = ExitStack()
    with ctx:
        def sb(name, shape, dt, where=ctx):
            return where.enter_context(nc.sbuf_tensor(name, shape, dt))

        def sem(name):
            return ctx.enter_context(nc.semaphore(name))

        raw_gu = sb("raw_gu", [P, 2, 2, H], f32)
        raw_d = sb("raw_d", [P, 2, H], f32)
        wgu = sb("wgu", [P, 2, 2, 2, H], f32r)
        xT = sb("xT", [P, 2, KT, TOK], f32r)
        wd = sb("wd", [P, FF * 2 * H], f32r)
        pb = sb("pb", [P, FF * 2 * PT], f32r)
        tok = sb("tok", [P, 4, H], f32)
        silu = sb("silu", [P, 2, CH], f32)
        tadd = sb("tadd", [32, 2, 2, PT], f32)
        tsum = sb("tsum", [32, 2, 2, PT], f32)
        own = sb("own", [32, 2], f32)
        ident = sb("ident", [P, P], f32)
        lnw = sb("lnw", [P, KT], f32)
        stat = sb("stat", [P, 8], f32)
        idx = sb("idx", [1, B], i32)
        with ExitStack() as early:
            act_c = sb("act_c", [P, FC * TOK], f32, early)
            ad = sb("ad", [P, FC, P], f32r, early)
            ad_raw = sb("ad_raw", [P, B, FC * RANK], f32, early)
        act_f = sb("act_f", [P, FF * TOK], f32)

        wd_t = wd[:, :].rearrange("p (t s h) -> p t s h", t=FF, s=2)
        pb_t = pb[:, :].rearrange("p (t s n) -> p t s n", t=FF, s=2)
        agu = wd[:, 9 * 2 * H:11 * 2 * H].rearrange("p (q k m) -> p q k m", q=PAIRS, k=KT)
        stack = wd[0:KS, 11 * 2 * H:13 * 2 * H].rearrange("p (y q m) -> p y q m", y=2, q=PAIRS)
        bgu = pb[:, 0:4 * FC * P].rearrange("p (s m) -> p s m", s=2)
        tgu01 = wd[0:KS, 13 * 2 * H:14 * 2 * H].rearrange("p (q g n) -> p q g n", q=2, g=2)
        tgu23 = pb[0:KS, 12 * 2 * PT:14 * 2 * PT].rearrange("p (q g n) -> p q g n", q=2, g=2)

        def tgu(q):
            return (tgu01 if q < 2 else tgu23)[:, q % 2]

        ad_hl = ad[:, :, :].rearrange("p t (s b r) -> p t s b r", s=2, b=4)
        agu_raw = act_c[:, 3 * TOK:4 * TOK].rearrange("p (b g k r) -> p b g k r", b=B, g=2, k=KT)
        bgu_raw = act_c[:, 4 * TOK:4 * TOK + 2 * FC * P]
        x_raw = act_c[:, 7 * TOK:11 * TOK].rearrange("p (k n) -> p k n", k=KT)
        bd_raw = raw_gu[CR:P, :, :, :].rearrange("p y g h -> p (y g) h")

        bank = [ctx.enter_context(nc.psum_tensor(f"bank{i}", [P, CH], f32)) for i in range(8)]
        T_BANK = bank[4]
        Y_BANK = [bank[5], bank[7]]
        TR_BANK = bank[6]
        Z_BANK = [bank[4], bank[5]]

        s_idx = sem("idx_loaded")
        s_lnw = sem("lnw_loaded")
        s_const = sem("consts_made")
        s_memset = sem("memset_done")
        s_x_ld = [[sem(f"x_loaded_{c}{k}") for k in range(KT if c == 0 else 2)] for c in range(2)]
        s_w0_ld = [sem("gate0_loaded"), sem("up0_loaded")]
        s_w_ld = [sem("w_loaded_even"), sem("w_loaded_odd")]
        s_wd_ld = [sem("wd_loaded_even"), sem("wd_loaded_odd")]
        s_agu_ld, s_bgu_ld = sem("agu_loaded"), [sem("bgu_loaded_0"), sem("bgu_loaded_1")]
        s_ad_ld, s_bd_ld = sem("ad_loaded"), sem("bd_loaded")
        s_st_a, s_st_v = sem("stack_by_scalar"), sem("stack_by_vector")
        s_hi = {n: sem(f"{n}_hi") for n in ("x", "w", "wd", "agu", "bgu", "ad", "bd", "act", "nx", "t")}
        s_split = {n: sem(f"{n}_split") for n in ("x", "w", "wd", "agu", "bgu", "ad", "bd", "act", "nx")}
        s_gate, s_up = sem("gate_ready"), sem("up_ready")
        s_silu, s_act = sem("silu_done"), sem("act_done")
        s_t, s_tadd, s_tsum, s_tsplit = (sem(n) for n in ("t_ready", "tadd_done", "tsum_done", "t_split"))
        s_pb_used = sem("act_pair_used")
        s_y = sem("y_ready")
        s_ss, s_var, s_std, s_inv = (sem(n) for n in ("squares_done", "var_done", "std_done", "inv_done"))
        s_newton = sem("newton_steps")
        s_warm = sem("warm_operand_made")
        s_y_taken = sem("y_taken")
        s_tr, s_nraw = sem("transposed"), sem("nraw_done")
        s_xr_ld, s_out = [sem("xrow_loaded_0"), sem("xrow_loaded_1")], [sem("out_stored_0"), sem("out_stored_1")]

        block = ctx.enter_context(nc.Block())

        def v32(ap):
            return ap.bitcast(f32)

        def w_loads(i, c):
            return i + (c + 1) // 2

        def wd_loads(i, c):
            return i + c // 2 + 1

        def over_tiles(eng, first, last, body):
            twos = (last - first + 1) // 2
            if twos > 1:
                with eng.Fori(0, twos) as i:
                    body(i, first)
                    body(i, first + 1)
                first += 2 * twos
            for c in range(first, last + 1):
                body(0, c)

        @block.sync
        def _(sp):
            def load_w(i, c):
                n = 2 * i + c
                if not (isinstance(n, int) and n < 2):
                    sp.wait_ge(s_split["w"], 2 * n - 2)
                sp.dma_start(raw_gu[:, c % 2, :, :], wgu_in[ds(n, 1), :, :].rearrange(
                    "o p (g f) -> (o p) g f", g=2)).then_inc(s_w_ld[c % 2], 16)

            def load_wd(i, c):
                n = 2 * i + c
                if not (isinstance(n, int) and n < 1):
                    sp.wait_ge(s_split["wd"], n)
                sp.dma_start(raw_d[:, c % 2, :], wd_in[ds(n, 1), :, :].rearrange(
                    "o p h -> (o p) h")).then_inc(s_wd_ld[c % 2], 16)

            sp.dma_start(idx[:, :], idx_in[:, :]).then_inc(s_idx, 16)
            sp.dma_start(raw_gu[:, 0, 0, :], wgu_in[0, :, 0:H]).then_inc(s_w0_ld[0], 16)
            for k in range(KT):
                sp.dma_start(x_raw[:, k, 0:CH], xT_in[:, k, 0:CH]).then_inc(s_x_ld[0][k], 16)
            sp.dma_start(raw_gu[:, 0, 1, :], wgu_in[0, :, H:2 * H]).then_inc(s_w0_ld[1], 16)
            for k in range(0, KT, 2):
                sp.dma_start(x_raw[:, k:k + 2, CH:TOK], xT_in[:, k:k + 2, CH:TOK]).then_inc(s_x_ld[1][k // 2], 16)
            sp.wait_ge(s_idx, 16)
            which = []
            for b in range(B):
                which.append(sp.value_load(idx[0:1, b:b + 1], min_val=0, max_val=R - 1))
                sp.dma_start(agu_raw[:, b], agu_in[ds(which[b], 1)].rearrange(
                    "o p (g k r) -> (o p) g k r", g=2, k=KT)).then_inc(s_agu_ld, 16)

            def load_b(part, lo, hi):
                for b in range(B):
                    sp.dma_start(bgu_raw[RANK * b:RANK * b + RANK, lo:hi],
                                 bgu_in[ds(which[b], 1), :, lo:hi].rearrange("o r m -> (o r) m")
                                 ).then_inc(s_bgu_ld[part], 16)

            load_b(0, 0, B_CUT)
            load_w(0, 1)
            load_b(1, B_CUT, 2 * FC * P)
            load_wd(0, 0)
            load_w(0, 2)
            load_wd(0, 1)
            sp.dma_start(lnw[:, :], lnw_in[:, :]).then_inc(s_lnw, 16)

            def tile_loads(i, c):
                load_w(i, c + 1)
                load_wd(i, c)

            over_tiles(sp, 2, FC - 2, tile_loads)
            load_w(0, FC)
            for b in range(B):
                sp.dma_start(ad_raw[:, b, :], ad_in[ds(which[b], 1)].rearrange("o p f -> (o p) f")
                             ).then_inc(s_ad_ld, 16)
            load_wd(0, FC - 1)
            sp.wait_ge(s_split["w"], 2 * FC + 2)
            for b in range(B):
                row = RANK * (b % 2)
                sp.dma_start(bd_raw[row:row + RANK, b // 2, :],
                             bd_in[ds(which[b], 1)].rearrange("o r h -> (o r) h")).then_inc(s_bd_ld, 16)
            sp.wait_ge(s_split["bd"], 2)
            load_w(0, FC + 1)
            load_wd(0, FC)
            sp.wait_ge(s_split["bd"], PAIRS)
            over_tiles(sp, FC + 1, NT - 2, tile_loads)
            load_wd(0, NT - 1)

            for t in range(2):
                sp.wait_ge(s_y_taken, 8)
                sp.dma_start(tok[:, 2 + t, :], x_in[t * P:t * P + P, :]).then_inc(s_xr_ld[t], 16)

            def store(q, t):
                sp.wait_ge(s_y_taken, 2 * q + t + 9)
                sp.dma_start(out[ds(q * PT + t * P, P), :], tok[:, 2 + t, :]).then_inc(s_out[t], 16)

            with sp.Fori(0, PAIRS - 1) as q:
                for t in range(2):
                    store(q, t)
                    sp.wait_ge(s_out[t], 16 * q + 16)
                    sp.dma_start(tok[:, 2 + t, :], x_in[ds(q * PT + PT + t * P, P), :]).then_inc(s_xr_ld[t], 16)
            for t in range(2):
                store(PAIRS - 1, t)
            for t in range(2):
                sp.wait_ge(s_out[t], 16 * PAIRS)

        @block.gpsimd
        def _(pool):
            nc.gpsimd.memset(ident[:, :], 0.0).then_inc(s_memset, 1)
            nc.gpsimd.memset(own[:, :], LORA_SCALE).then_inc(s_memset, 1)
            nc.gpsimd.memset(v32(ad[:, :, :]), 0.0).then_inc(s_const, 1)
            pool.wait_ge(s_memset, 2)
            nc.gpsimd.affine_select(out=ident[:, :], in_=ident[:, :], compare_op=ALU.not_equal, fill=1.0,
                                    base=0, pattern=[[-1, P]], channel_multiplier=1).then_inc(s_const, 1)
            nc.gpsimd.affine_select(out=own[:, 0:1], in_=own[:, 0:1], compare_op=ALU.is_ge, fill=0.0,
                                    base=RANK - 1, pattern=[[0, 1]], channel_multiplier=-1).then_inc(s_const, 1)
            nc.gpsimd.affine_select(out=own[:, 1:2], in_=own[:, 1:2], compare_op=ALU.is_ge, fill=0.0,
                                    base=-RANK, pattern=[[0, 1]], channel_multiplier=1).then_inc(s_const, 1)

        @block.scalar
        def _(a):
            def hi(name, out, raw):
                nc.scalar.activation(out, raw, ACT.Copy).then_inc(s_hi[name], 1)

            def hi_x(c):
                for k in range(KT):
                    if c == 0 or k % 2 == 0:
                        a.wait_ge(s_x_ld[c][k // (1 + c)], 16)
                    hi("x", xT[:, 0, k, c * CH:(c + 1) * CH], x_raw[:, k, c * CH:(c + 1) * CH])

            def hi_w(i, c):
                a.wait_ge(s_w_ld[c % 2], 16 * w_loads(i, c))
                if not (isinstance(i, int) and c < 2):
                    a.wait_ge(s_up, 4 * i + 2 * c - 2)
                for g in range(2):
                    hi("w", wgu[:, c % 2, g, 0, :], raw_gu[:, c % 2, g, :])

            def stack_b(i, c):
                for q in range(PAIRS):
                    ins = nc.scalar.activation(stack[0:32, c % 2, q], v32(bgu[32 * q:32 * q + 32, 0, ds(
                        (2 * i + c) * 2 * P, 2 * P)]), ACT.Copy)
                ins.then_inc(s_st_a, 1)

            def hi_wd(i, c, base, rows=P):
                a.wait_ge(s_wd_ld[c % 2], 16 * wd_loads(i, c))
                hi("wd", wd[0:rows, ds((2 * i + c - base) * 2 * H, H)], raw_d[0:rows, c % 2, :])

            def do_silu(i, c, chunk):
                n = 2 * i + c
                a.wait_ge(s_gate, 2 * n + chunk + 1)
                if not (isinstance(n, int) and n < 1):
                    a.wait_ge(s_act, 2 * n - 2 + chunk + 1)
                nc.scalar.activation(silu[:, chunk, :], bank[2 * chunk][:, :], ACT.Silu).then_inc(s_silu, 1)

            def t_parts(m, par, banks):
                a.wait_ge(s_t, m + 1)
                for j, (src, row) in enumerate(banks):
                    ins = nc.scalar.activation(tadd[:, par, j, :], src[row:row + 32, 0:PT], ACT.Copy)
                ins.then_inc(s_tadd, 1)

            def t_hi(m, par, k, out):
                a.wait_ge(s_tsum, m + 1)
                for b in range(2):
                    half = slice(b * P, b * P + P)
                    ins = nc.scalar.activation(out[:, :, half], tsum[:, par, 0:k, half], ACT.Copy,
                                               scale=own[:, b:b + 1])
                ins.then_inc(s_hi["t"], 1)

            def act_pair(q, tiles, act, before):
                last = (FF if act is act_f else FC) - 1
                for ft in tiles:
                    if before is not None and ft == last:
                        a.wait_ge(s_y, 2 * q + (8 if act is act_f else 0))
                    elif before is not None:
                        a.wait_ge(s_pb_used, before + ft + 1)
                    rows = CR if act is act_c and ft == FC - 1 else P
                    hi("act", pb_t[0:rows, ft, 0, :], act[0:rows, ds(q * PT + ft * TOK, PT)])

            def ad_pair(q):
                for b in range(2):
                    ins = nc.scalar.activation(ad_hl[:, :, 0, b, :], ad_raw[:, ds(2 * q + b, 1), :].rearrange(
                        "p o (t r) -> p (o t) r", r=RANK), ACT.Copy)
                ins.then_inc(s_hi["ad"], 1)

            a.wait_ge(s_warm, 2)
            nc.scalar.activation(stat[:, 1:2], stat[:, 0:1], ACT.Silu).then_inc(s_var, 1)
            a.wait_ge(s_w0_ld[0], 16)
            hi("w", wgu[:, 0, 0, 0, :], raw_gu[:, 0, 0, :])
            hi_x(0)
            a.wait_ge(s_w0_ld[1], 16)
            hi("w", wgu[:, 0, 1, 0, :], raw_gu[:, 0, 1, :])
            hi_x(1)
            a.wait_ge(s_agu_ld, 16 * B)
            agu_out = agu.rearrange("p q k (s g b r) -> p q k s g b r", s=2, g=2, b=2)
            agu_in4 = agu_raw.rearrange("p (q b) g k r -> p q b g k r", b=2)

            def t_gate_up(q):
                if q >= 2:
                    a.wait_ge(s_tsum, q - 1)
                t_parts(q, q % 2, [(bank[4 + q], 64), (bank[4 + q], 96)])

            def t_gate_up_hi(q):
                t_hi(q, q % 2, 2, tgu(q)[0:32])

            for g in range(2):
                for b in range(2):
                    hi("agu", agu_out[:, :, :, 0, g, b, :], agu_in4[:, :, b, g, :, :])
            a.wait_ge(s_const, 4)
            t_gate_up(0)
            t_gate_up(1)
            t_gate_up_hi(0)
            t_gate_up(2)
            t_gate_up_hi(1)
            a.wait_ge(s_bgu_ld[0], 16 * B)
            hi("bgu", bgu[:, 0, 0:B_CUT], bgu_raw[:, 0:B_CUT])
            a.wait_ge(s_hi["bgu"], 1)
            stack_b(0, 0)

            t_gate_up(3)
            t_gate_up_hi(2)
            t_gate_up_hi(3)
            hi_w(0, 1)
            do_silu(0, 0, 0)
            stack_b(0, 1)
            do_silu(0, 0, 1)
            a.wait_ge(s_bgu_ld[1], 16 * B)
            hi("bgu", bgu[:, 0, B_CUT:], bgu_raw[:, B_CUT:])
            hi_wd(0, 0, 0)
            a.wait_ge(s_hi["bgu"], 2)

            def tile(i, c, base):
                hi_w(i, c + 1)
                if base == 0:
                    stack_b(i, c + 1)
                hi_wd(i, c, base)
                do_silu(i, c, 0)
                do_silu(i, c, 1)

            over_tiles(a, 1, FC - 2, lambda i, c: tile(i, c, 0))
            hi_w(0, FC)
            hi_wd(0, FC - 1, 0, CR)
            do_silu(0, FC - 1, 0)
            a.wait_ge(s_st_a, FC)
            a.wait_ge(s_st_v, FC)
            a.wait_ge(s_ad_ld, 16 * B)
            ad_pair(0)
            a.wait_ge(s_act, 2 * FC - 1)
            act_pair(0, range(FC), act_c, None)
            do_silu(0, FC - 1, 1)
            a.wait_ge(s_bd_ld, 16 * B)

            def norm(q, t):
                m = 2 * q + t
                a.wait_ge(s_y, m + 1)
                nc.scalar.activation(silu[:, 0, :], Y_BANK[t][:, :], ACT.Square,
                                     accum_out=stat[:, 0:1]).then_inc(s_ss, 1)
                a.wait_ge(s_var, m + 2)
                nc.scalar.activation(stat[:, 2:3], stat[:, 1:2], ACT.Sqrt).then_inc(s_std, 1)

            def hi_nx(q, t):
                m = 2 * q + t
                a.wait_ge(s_nraw, m + 1)
                hi("nx", xT[:, 0, :, ds(m * P, P)], silu[:, 1, :].rearrange("p (k n) -> p k n", k=KT))

            def pair_b(q, last):
                t_parts(PAIRS + q, 0, [(T_BANK, 64)])
                hi("bd", wd_t[CR:P, FC - 1, 0, :], bd_raw[:, ds(q, 1), :].rearrange("p o h -> p (o h)"))
                t_hi(PAIRS + q, 0, 1, pb_t[CR:P, FC - 1, 0:1, :])
                if not last:
                    ad_pair(q + 1)
                    act_pair(q + 1, range(0, 4), act_c, q * (FC - 1))
                norm(q, 0)
                if not last:
                    act_pair(q + 1, range(4, FC), act_c, q * (FC - 1))
                norm(q, 1)
                hi_nx(q, 0)
                hi_nx(q, 1)

            with a.Fori(0, PAIRS - 1) as q:
                pair_b(q, False)
            pair_b(PAIRS - 1, True)

            do_silu(0, FC, 0)
            hi_w(0, FC + 1)
            hi_wd(0, FC, FC)
            do_silu(0, FC, 1)
            over_tiles(a, FC + 1, NT - 2, lambda i, c: tile(i, c, FC))
            hi_wd(0, NT - 1, FC)
            do_silu(0, NT - 1, 0)
            a.wait_ge(s_act, 2 * NT - 1)
            act_pair(0, range(FF), act_f, None)
            do_silu(0, NT - 1, 1)
            a.wait_ge(s_act, 2 * NT)
            with a.Fori(1, PAIRS) as q:
                act_pair(q, range(FF), act_f, PAIRS * (FC - 1) + (q - 1) * (FF - 1))

        @block.vector
        def _(v):
            def sub(out, raw, part):
                return nc.vector.tensor_tensor(out, raw, v32(part), ALU.subtract)

            def lo(name, count, out, raw, part):
                v.wait_ge(s_hi[name], count)
                sub(out, raw, part).then_inc(s_split[name], 1)

            def lo_x(c):
                for k in range(KT):
                    cols = slice(c * CH, (c + 1) * CH)
                    lo("x", KT * c + k + 1, xT[:, 1, k, cols], x_raw[:, k, cols], xT[:, 0, k, cols])

            def lo_w(i, c, g):
                lo("w", 4 * i + 2 * c + g + 1, wgu[:, c % 2, g, 1, :], raw_gu[:, c % 2, g, :],
                   wgu[:, c % 2, g, 0, :])

            def stack_b(i, c):
                if not (isinstance(i, int) and c < 2):
                    v.wait_ge(s_up, 4 * i + 2 * c - 2)
                for row, part in ((32, 1), (64, 0)):
                    for q in range(PAIRS):
                        ins = nc.vector.tensor_copy(stack[row:row + 32, c % 2, q], v32(bgu[
                            32 * q:32 * q + 32, part, ds((2 * i + c) * 2 * P, 2 * P)]))
                ins.then_inc(s_st_v, 1)

            def lo_wd(i, c, base, rows=P):
                n = 2 * i + c
                at = (n - base) * 2 * H
                lo("wd", n + 1, wd[0:rows, ds(at + H, H)], raw_d[0:rows, c % 2, :], wd[0:rows, ds(at, H)])

            def do_act(i, c, chunk, act, base):
                n = 2 * i + c
                v.wait_ge(s_up, 2 * n + chunk + 1)
                v.wait_ge(s_silu, 2 * n + chunk + 1)
                nc.vector.tensor_tensor(act[:, ds((n - base) * TOK + chunk * CH, CH)], silu[:, chunk, :],
                                        bank[2 * chunk + 1][:, :], ALU.mult).then_inc(s_act, 1)

            def t_sum(m, par, banks):
                v.wait_ge(s_tadd, m + 1)
                for j, (src, row) in enumerate(banks):
                    ins = nc.vector.tensor_tensor(tsum[:, par, j, :], src[row:row + 32, 0:PT],
                                                  tadd[:, par, j, :], ALU.add)
                ins.then_inc(s_tsum, 1)

            def t_lo(m, par, k, hi, out, copy=None):
                v.wait_ge(s_hi["t"], m + 1)
                if copy is not None:
                    nc.vector.tensor_copy(copy, v32(hi))
                for b in range(2):
                    half = slice(b * P, b * P + P)
                    ins = nc.vector.scalar_tensor_tensor(out[:, :, half], tsum[:, par, 0:k, half], own[:, b:b + 1],
                                                         v32(hi[:, :, half]), ALU.mult, ALU.subtract)
                ins.then_inc(s_tsplit, 1)

            def act_pair(q, tiles, act, count):
                for ft in tiles:
                    rows = CR if act is act_c and ft == FC - 1 else P
                    lo("act", count + ft + 1, pb_t[0:rows, ft, 1, :], act[0:rows, ds(q * PT + ft * TOK, PT)],
                       pb_t[0:rows, ft, 0, :])

            def ad_pair(q):
                v.wait_ge(s_hi["ad"], q + 1)
                for b in range(2):
                    ins = sub(ad_hl[:, :, 1, b, :], ad_raw[:, ds(2 * q + b, 1), :].rearrange(
                        "p o (t r) -> p (o t) r", r=RANK), ad_hl[:, :, 0, b, :])
                ins.then_inc(s_split["ad"], 1)

            nc.vector.memset(v32(pb[:, 0:2 * H]), 0.0).then_inc(s_warm, 1)
            nc.vector.memset(stat[:, :], 0.0).then_inc(s_warm, 1)
            lo_w(0, 0, 0)
            lo_x(0)
            lo_w(0, 0, 1)
            lo_x(1)
            agu_out = agu.rearrange("p q k (s g b r) -> p q k s g b r", s=2, g=2, b=2)
            agu_in4 = agu_raw.rearrange("p (q b) g k r -> p q b g k r", b=2)
            for g in range(2):
                for b in range(2):
                    lo("agu", 2 * g + b + 1, agu_out[:, :, :, 1, g, b, :], agu_in4[:, :, b, g, :, :],
                       agu_out[:, :, :, 0, g, b, :])
            v.wait_ge(s_const, 4)

            def t_gate_up(q):
                if q >= 2:
                    v.wait_ge(s_tsplit, q - 1)
                t_sum(q, q % 2, [(bank[4 + q], 0), (bank[4 + q], 32)])

            def t_gate_up_lo(q):
                t_lo(q, q % 2, 2, tgu(q)[0:32], tgu(q)[64:96], tgu(q)[32:64])

            t_gate_up(0)
            t_gate_up(1)
            t_gate_up_lo(0)
            t_gate_up(2)
            t_gate_up_lo(1)
            lo("bgu", 1, bgu[:, 1, 0:B_CUT], bgu_raw[:, 0:B_CUT], bgu[:, 0, 0:B_CUT])
            v.wait_ge(s_split["bgu"], 1)
            stack_b(0, 0)
            t_gate_up(3)
            t_gate_up_lo(2)
            t_gate_up_lo(3)
            lo_w(0, 1, 0)
            lo_w(0, 1, 1)
            do_act(0, 0, 0, act_c, 0)
            stack_b(0, 1)
            do_act(0, 0, 1, act_c, 0)
            lo("bgu", 2, bgu[:, 1, B_CUT:], bgu_raw[:, B_CUT:], bgu[:, 0, B_CUT:])
            lo_wd(0, 0, 0)
            v.wait_ge(s_split["bgu"], 2)

            def tile(i, c, act, base):
                lo_w(i, c + 1, 0)
                lo_w(i, c + 1, 1)
                if base == 0:
                    stack_b(i, c + 1)
                lo_wd(i, c, base)
                do_act(i, c, 0, act, base)
                do_act(i, c, 1, act, base)

            over_tiles(v, 1, FC - 2, lambda i, c: tile(i, c, act_c, 0))
            lo_w(0, FC, 0)
            lo_w(0, FC, 1)
            lo_wd(0, FC - 1, 0, CR)
            do_act(0, FC - 1, 0, act_c, 0)
            ad_pair(0)
            act_pair(0, range(FC), act_c, 0)
            do_act(0, FC - 1, 1, act_c, 0)
            v.wait_ge(s_lnw, 16)

            def norm(q, t):
                m = 2 * q + t
                v.wait_ge(s_ss, m + 1)
                nc.vector.tensor_scalar(stat[:, 1:2], stat[:, 0:1], 1.0 / H, NORM_EPS, ALU.mult, ALU.add
                                        ).then_inc(s_var, 1)
                v.wait_ge(s_std, m + 1)
                nc.vector.reciprocal(stat[:, 3:4], stat[:, 2:3]).then_inc(s_inv, 1)
                v.wait_ge(s_inv, m + 1)
                steps = [
                    lambda: nc.vector.tensor_scalar(stat[:, 4:5], stat[:, 3:4], stat[:, 3:4], stat[:, 1:2],
                                                    ALU.mult, ALU.mult),
                    lambda: nc.vector.tensor_scalar(stat[:, 5:6], stat[:, 4:5], -0.5, 1.5, ALU.mult, ALU.add),
                    lambda: nc.vector.tensor_tensor(stat[:, 6:7], stat[:, 3:4], stat[:, 5:6], ALU.mult),
                ]
                for k, step in enumerate(steps):
                    step().then_inc(s_newton, 1)
                    v.wait_ge(s_newton, 3 * m + k + 1)
                nc.vector.tensor_scalar(tok[:, t, :], Y_BANK[t][:, :], stat[:, 6:7], None, ALU.mult
                                        ).then_inc(s_y_taken, 1)

            def lo_nx(q, t):
                m = 2 * q + t
                raw = silu[:, 1, :].rearrange("p (k n) -> p k n", k=KT)
                v.wait_ge(s_tr, m + 1)
                if t == 1:
                    v.wait_ge(s_split["nx"], m)
                nc.vector.tensor_tensor(raw, TR_BANK[:, :].rearrange("p (k n) -> p k n", k=KT),
                                        lnw[:, :].unsqueeze(2).to_broadcast([P, KT, P]), ALU.mult
                                        ).then_inc(s_nraw, 1)
                lo("nx", m + 1, xT[:, 1, :, ds(m * P, P)], raw, xT[:, 0, :, ds(m * P, P)])

            def pair_b(q, last):
                t_sum(PAIRS + q, 0, [(T_BANK, 0)])
                lo("bd", q + 1, wd_t[CR:P, FC - 1, 1, :], bd_raw[:, ds(q, 1), :].rearrange("p o h -> p (o h)"),
                   wd_t[CR:P, FC - 1, 0, :])
                t_lo(PAIRS + q, 0, 1, pb_t[CR:P, FC - 1, 0:1, :], pb_t[CR:P, FC - 1, 1:2, :])
                if not last:
                    ad_pair(q + 1)
                    act_pair(q + 1, range(0, 4), act_c, (q + 1) * FC)
                norm(q, 0)
                if not last:
                    act_pair(q + 1, range(4, FC), act_c, (q + 1) * FC)
                norm(q, 1)
                lo_nx(q, 0)
                lo_nx(q, 1)

            with v.Fori(0, PAIRS - 1) as q:
                pair_b(q, False)
            pair_b(PAIRS - 1, True)

            do_act(0, FC, 0, act_f, FC)
            lo_w(0, FC + 1, 0)
            lo_w(0, FC + 1, 1)
            lo_wd(0, FC, FC)
            do_act(0, FC, 1, act_f, FC)
            over_tiles(v, FC + 1, NT - 2, lambda i, c: tile(i, c, act_f, FC))
            lo_wd(0, NT - 1, FC)
            do_act(0, NT - 1, 0, act_f, FC)
            act_pair(0, range(FF), act_f, PAIRS * FC)
            do_act(0, NT - 1, 1, act_f, FC)

            def add_x(q, t):
                v.wait_ge(s_xr_ld[t], 16 * q + 16)
                v.wait_ge(s_y, 2 * q + t + 9)
                nc.vector.tensor_tensor(tok[:, 2 + t, :], tok[:, 2 + t, :], Z_BANK[t][:, :], ALU.add
                                        ).then_inc(s_y_taken, 1)

            with v.Fori(0, PAIRS - 1) as q:
                add_x(q, 0)
                act_pair(q + 1, range(FF), act_f, PAIRS * FC + (q + 1) * FF)
                add_x(q, 1)
            add_x(PAIRS - 1, 0)
            add_x(PAIRS - 1, 1)

        @block.tensor
        def _(pe):
            mm = nc.tensor.matmul
            PASSES = ((0, 0), (0, 1), (1, 0))

            def project(par, g, chunk, lora, first=None, cols=(0, CH)):
                lo, hi = cols
                for k in range(KT):
                    if first is not None:
                        pe.wait_ge(s_split["x"], first + k)
                    for s, r in PASSES:
                        last = k == KT - 1 and s == 1 and not lora
                        ins = mm(bank[2 * chunk + g][:, lo:hi], wgu[:, par, g, s, k * P:(k + 1) * P],
                                 xT[:, r, k, chunk * CH + lo:chunk * CH + hi],
                                 start=(k == 0 and s == 0 and r == 0), stop=last)
                return ins

            def lora_gu(par, g, chunk):
                for q in (2 * chunk, 2 * chunk + 1):
                    half = (q % 2) * PT
                    ins = mm(bank[2 * chunk + g][:, half:half + PT], stack[:, par, q, g * P:(g + 1) * P], tgu(q)[:, g, :],
                             start=False, stop=(q % 2 == 1))
                ins.then_inc((s_gate, s_up)[g], 1)
                return ins

            def t_gate_up(q):
                for k in range(KT):
                    for r in range(2):
                        ins = mm(bank[4 + q][:, 0:PT], agu[:, q, k, :], xT[:, r, k, q * PT:(q + 1) * PT],
                                 start=(k == 0 and r == 0), stop=(k == KT - 1 and r == 1))
                ins.then_inc(s_t, 1)

            pe.wait_ge(s_warm, 1)
            for _ in range(WARM):
                mm(bank[3][:, :], pb[:, 0:P], pb[:, H:2 * H], start=True, stop=True)

            pe.wait_ge(s_split["w"], 1)
            project(0, 0, 0, True, first=1)
            pe.wait_ge(s_split["w"], 2)
            project(0, 1, 0, True)
            project(0, 0, 1, True, first=KT + 1)
            pe.wait_ge(s_split["agu"], 4)
            for q in range(PAIRS):
                t_gate_up(q)
            project(0, 1, 1, True)
            pe.wait_ge(s_st_a, 1)
            pe.wait_ge(s_st_v, 1)
            pe.wait_ge(s_tsplit, 2)
            lora_gu(0, 0, 0)
            lora_gu(0, 1, 0)
            pe.wait_ge(s_tsplit, 4)
            lora_gu(0, 0, 1)
            lora_gu(0, 1, 1)

            def tile(i, c, lora):
                n = 2 * i + c
                for chunk in range(2):
                    for g in range(2):
                        if chunk == 0:
                            pe.wait_ge(s_split["w"], 2 * n + g + 1)
                            if lora and g == 0:
                                pe.wait_ge(s_st_a, n + 1)
                                pe.wait_ge(s_st_v, n + 1)
                        pe.wait_ge((s_silu, s_act)[g], 2 * n - 2 + chunk + 1)
                        ins = project(c % 2, g, chunk, lora)
                        if lora:
                            ins = lora_gu(c % 2, g, chunk)
                        else:
                            ins.then_inc((s_gate, s_up)[g], 1)

            over_tiles(pe, 1, FC - 1, lambda i, c: tile(i, c, True))

            def down(z, ft, t, last):
                for s, r in PASSES:
                    ins = mm(z[:, :], pb_t[:, ft, s, t * P:(t + 1) * P], wd_t[:, ft, r, :],
                             start=(ft == 0 and s == 0 and r == 0), stop=(ft == last and s == 1))
                return ins

            def transposes(q, t):
                pe.wait_ge(s_y_taken, 2 * q + t + 1)
                if t == 1:
                    pe.wait_ge(s_nraw, 2 * q + 1)
                for k in range(KT):
                    ins = nc.tensor.transpose(TR_BANK[:, k * P:(k + 1) * P], tok[:, t, k * P:(k + 1) * P],
                                              ident[:, :])
                ins.then_inc(s_tr, 1)

            def pair_b(q, first):
                if not first:
                    pe.wait_ge(s_y_taken, 2 * q - 1)
                for ft in range(FC):
                    pe.wait_ge(s_split["act"], q * FC + ft + 1)
                    if ft == 0:
                        pe.wait_ge(s_split["ad"], q + 1)
                    rows = CR if ft == FC - 1 else P
                    for r in range(2):
                        ins = mm(T_BANK[:, 0:PT], ad[0:rows, ft, :], pb_t[0:rows, ft, r, :],
                                 start=(ft == 0 and r == 0), stop=(ft == FC - 1 and r == 1))
                    if ft == FC - 1:
                        ins.then_inc(s_t, 1)
                    else:
                        down(Y_BANK[0], ft, 0, FC - 1)
                    if ft in (2, 7) and not first:
                        transposes(q - 1, int(ft == 7))
                for ft in range(FC - 1):
                    down(Y_BANK[1], ft, 1, FC - 1).then_inc(s_pb_used, 1)
                    if ft == 4:
                        pe.wait_ge(s_split["bd"], q + 1)
                        pe.wait_ge(s_tsplit, PAIRS + q + 1)
                        down(Y_BANK[0], FC - 1, 0, FC - 1).then_inc(s_y, 1)
                down(Y_BANK[1], FC - 1, 1, FC - 1).then_inc(s_y, 1)

            pe.wait_ge(s_split["wd"], FC)
            pe.wait_ge(s_const, 4)
            pair_b(0, True)
            with pe.Fori(1, PAIRS) as q:
                pair_b(q, False)

            pe.wait_ge(s_split["nx"], 4)
            for g in range(2):
                pe.wait_ge(s_split["w"], 2 * FC + g + 1)
                project(FC % 2, g, 0, False).then_inc((s_gate, s_up)[g], 1)
                transposes(PAIRS - 1, g)
            pe.wait_ge(s_split["nx"], 6)
            for g in range(2):
                project(FC % 2, g, 1, False, cols=(0, PT))
            pe.wait_ge(s_split["nx"], 8)
            for g in range(2):
                project(FC % 2, g, 1, False, cols=(PT, CH)).then_inc((s_gate, s_up)[g], 1)
            over_tiles(pe, FC + 1, NT - 1, lambda i, c: tile(i, c, False))

            pe.wait_ge(s_split["wd"], NT)
            with pe.Fori(0, PAIRS) as q:
                for t in range(2):
                    pe.wait_ge(s_y_taken, 2 * q + t + 7)
                    for ft in range(FF):
                        if t == 0:
                            pe.wait_ge(s_split["act"], PAIRS * FC + q * FF + ft + 1)
                        ins = down(Z_BANK[t], ft, t, FF - 1)
                        if ft == FF - 1:
                            ins.then_inc(s_y, 1)
                        elif t == 1:
                            ins.then_inc(s_pb_used, 1)


def kernel(**inputs):
    import numpy as np
    import concourse.bacc as bacc
    from concourse.bass_utils import run_bass_kernel_spmd

    def arr(name):
        return np.asarray(inputs[name])

    def pad_rows(w, rows):
        return np.concatenate([w, np.zeros((rows - w.shape[0],) + w.shape[1:], w.dtype)], 0)

    def gate_up(gate, up, tiles):
        both = np.stack([pad_rows(gate, tiles * P), pad_rows(up, tiles * P)])
        return both.reshape(2, tiles, P, KT, P).transpose(1, 4, 0, 3, 2).reshape(tiles, P, 2 * H)

    def down(w, tiles):
        return pad_rows(w.T, tiles * P).reshape(tiles, P, H)

    x = arr("x").reshape(TOK, H)
    a_gu = np.stack([arr("L0_cond_A_gate")[0], arr("L0_cond_A_up")[0]])
    b_gu = np.stack([arr("L0_cond_B_gate")[0], arr("L0_cond_B_up")[0]])
    b_gu = np.concatenate([b_gu, np.zeros((2, R, FC * P - b_gu.shape[2], RANK), b_gu.dtype)], 2)
    a_d = arr("L0_cond_A_down")[0]
    a_d = np.concatenate([a_d, np.zeros((R, RANK, FC * P - a_d.shape[2]), a_d.dtype)], 2)
    feeds = {
        "xT_in": x.T.reshape(KT, P, TOK).transpose(1, 0, 2),
        "x_in": x,
        "idx_in": arr("itok_B_2_6").reshape(1, B),
        "wgu_in": np.concatenate([gate_up(arr("L0_cond_W_gate"), arr("L0_cond_W_up"), FC),
                                  gate_up(arr("L0_ffn_gate_w"), arr("L0_ffn_up_w"), FF)], 0),
        "wd_in": np.concatenate([down(arr("L0_cond_W_down"), FC), down(arr("L0_ffn_down_w"), FF)], 0),
        "agu_in": a_gu.reshape(2, R, RANK, KT, P).transpose(1, 4, 0, 3, 2).reshape(R, P, 2 * KT * RANK),
        "bgu_in": b_gu.reshape(2, R, FC, P, RANK).transpose(1, 4, 2, 0, 3).reshape(R, RANK, 2 * FC * P),
        "ad_in": a_d.reshape(R, RANK, FC, P).transpose(0, 3, 2, 1).reshape(R, P, FC * RANK),
        "bd_in": arr("L0_cond_B_down")[0].transpose(0, 2, 1),
        "lnw_in": arr("L0_ffn_ln_w").reshape(KT, P).T,
    }
    feeds = {k: np.ascontiguousarray(v) for k, v in feeds.items()}
    nc = bacc.Bacc("TRN2", target_bir_lowering=False, num_devices=1, dynamic_dma_scratch_size=1024)
    args = [nc.dram_tensor(k, v.shape, mybir.dt.from_np(v.dtype), kind="ExternalInput").ap()
            for k, v in feeds.items()]
    out = nc.dram_tensor("out", (TOK, H), mybir.dt.float32, kind="ExternalOutput").ap()
    build(nc, *args, out)
    r = run_bass_kernel_spmd(nc, [feeds], core_ids=[0])
    return r.results[0]["out"].reshape(B, P, H)
```

```python
from contextlib import ExitStack

import concourse.bass as bass
from concourse import mybir

TOK, H, R, RANK, B = 1024, 512, 16, 16, 8
P = 128
KT = H // P
FC, FF = 11, 14
NT = FC + FF
PAIRS = B // 2
CH = 512
PT = 2 * P
KS = 96
CR = 1376 - (FC - 1) * P
SHORT = 1
ORDER_B = [ft for ft in range(FC) if ft != SHORT] + [SHORT]
ORDER_E = list(range(FF))
NORM_EPS = 1e-5
LORA_SCALE = 0.5
WARM = 12
B_CUTS = (0, 3 * 2 * P, 5 * 2 * P, FC * 2 * P)


def build(nc, xT_in, x_in, idx_in, wgu_in, wd_in, agu_in, bgu_in, ad_in, bd_in, lnw_in, out):
    f32, f32r, i32 = mybir.dt.float32, mybir.dt.float32r, mybir.dt.int32
    ALU, ACT = mybir.AluOpType, mybir.ActivationFunctionType
    ds = bass.ds
    ctx = ExitStack()
    with ctx:
        def sb(name, shape, dt, where=ctx):
            return where.enter_context(nc.sbuf_tensor(name, shape, dt))

        def sem(name):
            return ctx.enter_context(nc.semaphore(name))

        raw_gu = sb("raw_gu", [P, 2, 2, H], f32)
        raw_d = sb("raw_d", [P, 2, H], f32)
        wgu = sb("wgu", [P, 2, 2, 2, H], f32r)
        xT = sb("xT", [P, 2, KT, TOK], f32r)
        wd = sb("wd", [P, FF * 2 * H], f32r)
        pb = sb("pb", [P, FF * 2 * PT], f32r)
        tok = sb("tok", [P, 4, H], f32)
        silu = sb("silu", [P, 2, CH], f32)
        tadd = sb("tadd", [32, PT], f32)
        tsum = sb("tsum", [32, PT], f32)
        own = sb("own", [P, 4], f32)
        ident = sb("ident", [P, P], f32)
        lnw = sb("lnw", [P, KT], f32)
        stat = sb("stat", [P, 8], f32)
        idx = sb("idx", [1, B], i32)
        with ExitStack() as early:
            act_c = sb("act_c", [P, FC * TOK], f32, early)
            ad = sb("ad", [P, FC, P], f32r, early)
            ad_raw = sb("ad_raw", [P, B, FC * RANK], f32, early)
        act_f = sb("act_f", [P, FF * TOK], f32)

        wd_t = wd[:, :].rearrange("p (t s h) -> p t s h", t=FF, s=2)
        pb_t = pb[:, :].rearrange("p (t s n) -> p t s n", t=FF, s=2)
        wsh = wd[:, 3 * 2 * H:11 * 2 * H].rearrange("p (q g s k m) -> p q g s k m", q=PAIRS, g=2, s=2, k=KT)
        stack = wd[0:KS, 11 * 2 * H:13 * 2 * H].rearrange("p (y q m) -> p y q m", y=2, q=PAIRS)
        bgu = pb[:, 0:4 * FC * P].rearrange("p (s m) -> p s m", s=2)
        tgu01 = wd[0:KS, 13 * 2 * H:14 * 2 * H].rearrange("p (q g n) -> p q g n", q=2, g=2)
        tgu23 = pb[0:KS, 12 * 2 * PT:14 * 2 * PT].rearrange("p (q g n) -> p q g n", q=2, g=2)

        tgu_chunk = (tgu01, tgu23)

        def tgu(q):
            return tgu_chunk[q // 2][:, q % 2]

        def t_rows(chunk, row, g, b):
            return tgu_chunk[chunk][row:row + 32, :, g, b * P:b * P + P]

        ad_hl = ad[:, :, :].rearrange("p t (s b r) -> p t s b r", s=2, b=4)
        agu_raw = act_c[:, 3 * TOK:4 * TOK].rearrange("p (b g k r) -> p b g k r", b=B, g=2, k=KT)
        bgu_raw = act_c[:, 4 * TOK:4 * TOK + 2 * FC * P]
        x_raw = act_c[:, 7 * TOK:11 * TOK].rearrange("p (k n) -> p k n", k=KT)
        bd_raw = raw_gu[CR:P, :, :, :].rearrange("p y g h -> p (y g) h")

        bank = [ctx.enter_context(nc.psum_tensor(f"bank{i}", [P, CH], f32)) for i in range(8)]
        T_BANK = bank[4]
        Y_BANK = [bank[5], bank[7]]
        TR_BANK = bank[6]
        Z_BANK = [bank[4], bank[5]]
        HALF_BANK = [bank[6], bank[7]]

        def t_psum(chunk, g, b):
            return bank[4 + 2 * chunk + g][CR:P, :].rearrange("p (q b n) -> p q b n", q=2, b=2)[:, :, b, :]

        s_idx = sem("idx_loaded")
        s_lnw = sem("lnw_loaded")
        s_const = sem("consts_made")
        s_memset = sem("memset_done")
        s_x_ld = [[sem(f"x_loaded_{c}{k}") for k in range(KT if c == 0 else 2)] for c in range(2)]
        s_w0_ld = [sem("gate0_loaded"), sem("up0_loaded")]
        s_w_ld = [sem("w_loaded_even"), sem("w_loaded_odd")]
        s_wd_ld = [sem("wd_loaded_even"), sem("wd_loaded_odd")]
        s_agu_ld, s_bgu_ld = [sem(f"agu_loaded_{q}") for q in range(PAIRS)], [sem("bgu_loaded_0"), sem("bgu_loaded_1")]
        s_ad_ld, s_bd_ld = sem("ad_loaded"), sem("bd_loaded")
        s_st_a, s_st_v = sem("stack_by_scalar"), sem("stack_by_vector")
        s_hi = {n: sem(f"{n}_hi") for n in ("x", "w", "wd", "agu", "bgu", "ad", "bd", "act", "nx", "t")}
        s_split = {n: sem(f"{n}_split") for n in ("x", "w", "wd", "agu", "bgu", "ad", "bd", "act", "nx")}
        s_gate, s_up = sem("gate_ready"), sem("up_ready")
        s_silu, s_act = sem("silu_done"), sem("act_done")
        s_t, s_tadd, s_tsum, s_tsplit = (sem(n) for n in ("t_ready", "tadd_done", "tsum_done", "t_split"))
        s_pb_used = sem("act_pair_used")
        s_y = sem("y_ready")
        s_ss, s_var, s_std, s_inv = (sem(n) for n in ("squares_done", "var_done", "std_done", "inv_done"))
        s_newton = sem("newton_steps")
        s_warm = sem("warm_operand_made")
        s_tcopy = sem("t_copied")
        s_proj0 = sem("tile_0_projected")
        s_kept = [sem("short_chunk_0_kept"), sem("short_chunk_1_kept")]
        s_gsum, s_usum = sem("short_gate_summed"), sem("short_up_summed")
        s_y_taken = sem("y_taken")
        s_tr, s_nraw = sem("transposed"), sem("nraw_done")
        s_xr_ld, s_out = [sem("xrow_loaded_0"), sem("xrow_loaded_1")], [sem("out_stored_0"), sem("out_stored_1")]

        block = ctx.enter_context(nc.Block())

        HALVES = (slice(0, H // 2), slice(H // 2, H))

        def v32(ap):
            return ap.bitcast(f32)

        short_raw = raw_gu[:, 1, :, :].rearrange("p g (k m) -> p g k m", k=KT)[:, :, :, 0:CR]

        kept = act_c[0:CR, TOK:3 * TOK].rearrange("p (g n) -> p g n", g=2)

        def a_part(b, part):
            col = CR + RANK * (b % 2)
            return wsh[:, b // 2, :, part, :, col:col + RANK]

        def w_loads(i, c):
            return i + (c + 1) // 2

        def wd_loads(i, c):
            return i + c // 2 + 1

        def over_tiles(eng, first, last, body):
            twos = (last - first + 1) // 2
            if twos > 1:
                with eng.Fori(0, twos) as i:
                    body(i, first)
                    body(i, first + 1)
                first += 2 * twos
            for c in range(first, last + 1):
                body(0, c)

        @block.sync
        def _(sp):
            def load_w(i, c):
                n = 2 * i + c
                if isinstance(n, int) and n == 2:
                    sp.wait_ge(s_split["w"], 2)
                elif not (isinstance(n, int) and n < 2):
                    sp.wait_ge(s_split["w"], 2 * n)
                sp.dma_start(raw_gu[:, c % 2, :, :], wgu_in[ds(n, 1), :, :].rearrange(
                    "o p (g f) -> (o p) g f", g=2)).then_inc(s_w_ld[c % 2], 16)

            def load_wd(i, c):
                n = 2 * i + c
                if not (isinstance(n, int) and n < 2):
                    sp.wait_ge(s_split["wd"], n - 1)
                sp.dma_start(raw_d[:, c % 2, :], wd_in[ds(n, 1), :, :].rearrange(
                    "o p h -> (o p) h")).then_inc(s_wd_ld[c % 2], 16)

            sp.dma_start(idx[:, :], idx_in[:, :]).then_inc(s_idx, 16)
            sp.dma_start(raw_gu[:, 0, 0, :], wgu_in[0, :, 0:H]).then_inc(s_w0_ld[0], 16)
            for k in range(KT):
                sp.dma_start(x_raw[:, k, 0:CH], xT_in[:, k, 0:CH]).then_inc(s_x_ld[0][k], 16)
            sp.dma_start(raw_gu[:, 0, 1, :], wgu_in[0, :, H:2 * H]).then_inc(s_w0_ld[1], 16)
            for k in range(0, KT, 2):
                sp.dma_start(x_raw[:, k:k + 2, CH:TOK], xT_in[:, k:k + 2, CH:TOK]).then_inc(s_x_ld[1][k // 2], 16)
            load_w(0, 1)
            sp.wait_ge(s_idx, 16)
            which = []
            for b in range(B):
                which.append(sp.value_load(idx[0:1, b:b + 1], min_val=0, max_val=R - 1))
                sp.dma_start(agu_raw[:, b], agu_in[ds(which[b], 1)].rearrange(
                    "o p (g k r) -> (o p) g k r", g=2, k=KT)).then_inc(s_agu_ld[b // 2], 16)

            def load_b(part, lo, hi):
                for b in range(B):
                    sp.dma_start(bgu_raw[RANK * b:RANK * b + RANK, lo:hi],
                                 bgu_in[ds(which[b], 1), :, lo:hi].rearrange("o r m -> (o r) m")
                                 ).then_inc(s_bgu_ld[part], 16)

            load_w(0, 2)
            load_b(0, 0, B_CUTS[1])
            load_b(1, B_CUTS[1], B_CUTS[3])
            load_wd(0, 0)
            load_wd(0, 1)
            sp.dma_start(lnw[:, :], lnw_in[:, :]).then_inc(s_lnw, 16)

            def tile_loads(i, c):
                load_w(i, c + 1)
                load_wd(i, c)

            over_tiles(sp, 2, FC - 2, tile_loads)
            load_w(0, FC)
            for b in range(B):
                sp.dma_start(ad_raw[:, b, :], ad_in[ds(which[b], 1)].rearrange("o p f -> (o p) f")
                             ).then_inc(s_ad_ld, 16)
            load_wd(0, FC - 1)
            sp.wait_ge(s_split["w"], 2 * FC + 4)
            for b in range(B):
                row = RANK * (b % 2)
                sp.dma_start(bd_raw[row:row + RANK, b // 2, :],
                             bd_in[ds(which[b], 1)].rearrange("o r h -> (o r) h")).then_inc(s_bd_ld, 16)
            sp.wait_ge(s_split["bd"], 2)
            load_w(0, FC + 1)
            load_wd(0, FC)
            sp.wait_ge(s_split["bd"], PAIRS)
            over_tiles(sp, FC + 1, NT - 2, tile_loads)
            load_wd(0, NT - 1)

            for t in range(2):
                sp.wait_ge(s_y_taken, 8)
                sp.dma_start(tok[:, 2 + t, :], x_in[t * P:t * P + P, :]).then_inc(s_xr_ld[t], 16)

            def store(q, t):
                sp.wait_ge(s_y_taken, 2 * q + t + 9)
                sp.dma_start(out[ds(q * PT + t * P, P), :], tok[:, 2 + t, :]).then_inc(s_out[t], 16)

            with sp.Fori(0, PAIRS - 1) as q:
                for t in range(2):
                    store(q, t)
                    sp.wait_ge(s_out[t], 16 * q + 16)
                    sp.dma_start(tok[:, 2 + t, :], x_in[ds(q * PT + PT + t * P, P), :]).then_inc(s_xr_ld[t], 16)
            store(PAIRS - 1, 0)
            for h, cols in enumerate(HALVES):
                sp.wait_ge(s_y_taken, 4 * PAIRS + h)
                sp.dma_start(out[TOK - P:TOK, cols], tok[:, 3, cols]).then_inc(s_out[1], 16)
            for t in range(2):
                sp.wait_ge(s_out[t], 16 * (PAIRS + t))

        @block.gpsimd
        def _(pool):
            nc.gpsimd.memset(ident[:, :], 0.0).then_inc(s_memset, 1)
            nc.gpsimd.memset(own[:, :], LORA_SCALE).then_inc(s_memset, 1)
            nc.gpsimd.memset(v32(ad[:, :, :]), 0.0).then_inc(s_const, 1)
            pool.wait_ge(s_memset, 2)
            nc.gpsimd.affine_select(out=ident[:, :], in_=ident[:, :], compare_op=ALU.not_equal, fill=1.0,
                                    base=0, pattern=[[-1, P]], channel_multiplier=1).then_inc(s_const, 1)
            for col, row in ((0, 0), (2, CR)):
                first, second = own[:, col:col + 1], own[:, col + 1:col + 2]
                nc.gpsimd.affine_select(out=first, in_=first, compare_op=ALU.is_ge, fill=0.0, base=row + RANK - 1,
                                        pattern=[[0, 1]], channel_multiplier=-1).then_inc(s_const, 1)
                nc.gpsimd.affine_select(out=second, in_=second, compare_op=ALU.is_ge, fill=0.0, base=-row - RANK,
                                        pattern=[[0, 1]], channel_multiplier=1).then_inc(s_const, 1)

        @block.scalar
        def _(a):
            def hi(name, out, raw):
                nc.scalar.activation(out, raw, ACT.Copy).then_inc(s_hi[name], 1)

            def hi_x(c):
                for k in range(KT):
                    if c == 0 or k % 2 == 0:
                        a.wait_ge(s_x_ld[c][k // (1 + c)], 16)
                    hi("x", xT[:, 0, k, c * CH:(c + 1) * CH], x_raw[:, k, c * CH:(c + 1) * CH])

            def hi_w(i, c):
                a.wait_ge(s_w_ld[c % 2], 16 * w_loads(i, c))
                if not (isinstance(i, int) and c <= 2):
                    a.wait_ge(s_up, 4 * i + 2 * c - 2)
                for g in range(2):
                    hi("w", wgu[:, c % 2, g, 0, :], raw_gu[:, c % 2, g, :])

            def stack_b(i, c):
                for q in range(PAIRS):
                    ins = nc.scalar.activation(stack[0:32, c % 2, q], v32(bgu[32 * q:32 * q + 32, 0, ds(
                        (2 * i + c) * 2 * P, 2 * P)]), ACT.Copy)
                ins.then_inc(s_st_a, 1)

            def hi_b(part):
                cols = slice(B_CUTS[part], B_CUTS[part + 1])
                if part < 2:
                    a.wait_ge(s_bgu_ld[part], 16 * B)
                hi("bgu", bgu[:, 0, cols], bgu_raw[:, cols])

            def hi_wd(i, c, base, rows=P):
                a.wait_ge(s_wd_ld[c % 2], 16 * wd_loads(i, c))
                hi("wd", wd[0:rows, ds((2 * i + c - base) * 2 * H, H)], raw_d[0:rows, c % 2, :])

            def do_silu(i, c, chunk):
                n = 2 * i + c
                a.wait_ge(s_gate, 2 * n + chunk + 1)
                if not (isinstance(n, int) and n < 1):
                    a.wait_ge(s_act, 2 * n - 2 + chunk + 1)
                nc.scalar.activation(silu[:, chunk, :], bank[2 * chunk][:, :], ACT.Silu).then_inc(s_silu, 1)

            def t_gate_up(chunk):
                for g in range(2):
                    a.wait_ge(s_t, 4 * chunk + g + 3)
                    for b in range(2):
                        ins = nc.scalar.activation(t_rows(chunk, 0, g, b), t_psum(chunk, g, b), ACT.Copy,
                                                   scale=own[CR:P, b + 2:b + 3])
                    ins.then_inc(s_hi["t"], 1)
                a.wait_ge(s_hi["t"], 2 * chunk + 2)
                nc.scalar.activation(tgu_chunk[chunk][32:64], v32(tgu_chunk[chunk][0:32]), ACT.Copy
                                     ).then_inc(s_tcopy, 1)

            def act_pair(q, places, act, before):
                order = ORDER_E if act is act_f else ORDER_B
                for at in places:
                    ft = order[at]
                    if before is not None and at == len(order) - 1:
                        a.wait_ge(s_y, 2 * q + (8 if act is act_f else 0))
                    elif before is not None:
                        a.wait_ge(s_pb_used, before + at + 1)
                    rows = CR if act is act_c and ft == SHORT else P
                    hi("act", pb_t[0:rows, ft, 0, :], act[0:rows, ds(q * PT + ft * TOK, PT)])

            def ad_pair(q):
                for b in range(2):
                    ins = nc.scalar.activation(ad_hl[:, :, 0, b, :], ad_raw[:, ds(2 * q + b, 1), :].rearrange(
                        "p o (t r) -> p (o t) r", r=RANK), ACT.Copy)
                ins.then_inc(s_hi["ad"], 1)

            a.wait_ge(s_warm, 2)
            nc.scalar.activation(stat[:, 1:2], stat[:, 0:1], ACT.Silu).then_inc(s_var, 1)
            a.wait_ge(s_w0_ld[0], 16)
            hi("w", wgu[:, 0, 0, 0, :], raw_gu[:, 0, 0, :])
            hi_x(0)
            a.wait_ge(s_w0_ld[1], 16)
            hi("w", wgu[:, 0, 1, 0, :], raw_gu[:, 0, 1, :])
            hi_x(1)

            def hi_short(q):
                a.wait_ge(s_w_ld[1], 16)
                hi("w", wsh[:, q, :, 0, :, 0:CR], short_raw)
                a.wait_ge(s_agu_ld[q], 32)
                for b in (2 * q, 2 * q + 1):
                    hi("agu", a_part(b, 0), agu_raw[:, b])

            for q in range(PAIRS):
                hi_short(q)
            a.wait_ge(s_proj0, 1)
            hi_w(0, 2)

            def short_silu(chunk):
                a.wait_ge(s_gsum, chunk + 1)
                a.wait_ge(s_act, chunk + 1)
                nc.scalar.activation(silu[0:CR, chunk, :], kept[:, 0, chunk * CH:chunk * CH + CH], ACT.Silu
                                     ).then_inc(s_silu, 1)

            hi_b(0)
            a.wait_ge(s_hi["bgu"], 1)
            stack_b(0, 0)
            a.wait_ge(s_const, 6)
            t_gate_up(0)
            stack_b(0, 1)
            do_silu(0, 0, 0)
            hi_wd(0, 0, 0)
            hi_wd(0, 1, 0, CR)
            t_gate_up(1)
            for g in range(2):
                ins = nc.scalar.activation(kept[:, g, CH:TOK], bank[6 + g][0:CR, :], ACT.Copy)
            ins.then_inc(s_kept[1], 1)
            a.wait_ge(s_up, 2)
            stack_b(0, 2)
            do_silu(0, 0, 1)
            hi_b(1)
            short_silu(0)
            short_silu(1)

            def tile(i, c, base):
                hi_w(i, c + 1)
                if base == 0:
                    stack_b(i, c + 1)
                hi_wd(i, c, base)
                do_silu(i, c, 0)
                do_silu(i, c, 1)

            a.wait_ge(s_hi["bgu"], 2)
            tile(0, 2, 0)
            hi_b(2)
            a.wait_ge(s_hi["bgu"], 3)
            over_tiles(a, 3, FC - 2, lambda i, c: tile(i, c, 0))
            hi_w(0, FC)
            hi_wd(0, FC - 1, 0)
            do_silu(0, FC - 1, 0)
            a.wait_ge(s_st_a, FC)
            a.wait_ge(s_st_v, FC)
            a.wait_ge(s_ad_ld, 16 * B)
            ad_pair(0)
            a.wait_ge(s_act, 2 * FC - 1)
            act_pair(0, range(FC), act_c, None)
            do_silu(0, FC - 1, 1)
            a.wait_ge(s_bd_ld, 16 * B)

            def norm(q, t):
                m = 2 * q + t
                a.wait_ge(s_y, m + 1)
                nc.scalar.activation(silu[:, 0, :], Y_BANK[t][:, :], ACT.Square,
                                     accum_out=stat[:, 0:1]).then_inc(s_ss, 1)
                a.wait_ge(s_var, m + 2)
                nc.scalar.activation(stat[:, 2:3], stat[:, 1:2], ACT.Sqrt).then_inc(s_std, 1)

            def hi_nx(q, t):
                m = 2 * q + t
                a.wait_ge(s_nraw, m + 1)
                hi("nx", xT[:, 0, :, ds(m * P, P)], silu[:, 1, :].rearrange("p (k n) -> p k n", k=KT))

            def pair_b(q, last):
                a.wait_ge(s_t, 2 * PAIRS + q + 1)
                nc.scalar.activation(tadd[:, :], T_BANK[64:96, 0:PT], ACT.Copy).then_inc(s_tadd, 1)
                hi("bd", wd_t[CR:P, SHORT, 0, :], bd_raw[:, ds(q, 1), :].rearrange("p o h -> p (o h)"))
                a.wait_ge(s_tsum, q + 1)
                for b in range(2):
                    half = slice(b * P, b * P + P)
                    ins = nc.scalar.activation(pb_t[CR:P, SHORT, 0, half], tsum[:, half], ACT.Copy,
                                               scale=own[0:32, b:b + 1])
                ins.then_inc(s_hi["t"], 1)
                if not last:
                    ad_pair(q + 1)
                    act_pair(q + 1, range(0, 4), act_c, q * (FC - 1))
                norm(q, 0)
                if not last:
                    act_pair(q + 1, range(4, FC), act_c, q * (FC - 1))
                norm(q, 1)
                hi_nx(q, 0)
                hi_nx(q, 1)

            with a.Fori(0, PAIRS - 1) as q:
                pair_b(q, False)
            pair_b(PAIRS - 1, True)

            do_silu(0, FC, 0)
            hi_w(0, FC + 1)
            hi_wd(0, FC, FC)
            do_silu(0, FC, 1)
            over_tiles(a, FC + 1, NT - 2, lambda i, c: tile(i, c, FC))
            hi_wd(0, NT - 1, FC)
            do_silu(0, NT - 1, 0)
            a.wait_ge(s_act, 2 * NT - 1)
            act_pair(0, range(FF), act_f, None)
            do_silu(0, NT - 1, 1)
            a.wait_ge(s_act, 2 * NT)
            with a.Fori(1, PAIRS) as q:
                act_pair(q, range(FF), act_f, PAIRS * (FC - 1) + (q - 1) * (FF - 1))

        @block.vector
        def _(v):
            def sub(out, raw, part):
                return nc.vector.tensor_tensor(out, raw, v32(part), ALU.subtract)

            def lo(name, count, out, raw, part):
                v.wait_ge(s_hi[name], count)
                sub(out, raw, part).then_inc(s_split[name], 1)

            def lo_x(c):
                for k in range(KT):
                    cols = slice(c * CH, (c + 1) * CH)
                    lo("x", KT * c + k + 1, xT[:, 1, k, cols], x_raw[:, k, cols], xT[:, 0, k, cols])

            def lo_w(i, c, g):
                count = 4 * i + 2 * c + g + (1 if isinstance(i, int) and c == 0 else 3)
                lo("w", count, wgu[:, c % 2, g, 1, :], raw_gu[:, c % 2, g, :],
                   wgu[:, c % 2, g, 0, :])

            def stack_b(i, c):
                if not (isinstance(i, int) and c < 2):
                    v.wait_ge(s_up, 4 * i + 2 * c - 2)
                for row, part in ((32, 1), (64, 0)):
                    for q in range(PAIRS):
                        ins = nc.vector.tensor_copy(stack[row:row + 32, c % 2, q], v32(bgu[
                            32 * q:32 * q + 32, part, ds((2 * i + c) * 2 * P, 2 * P)]))
                ins.then_inc(s_st_v, 1)

            def lo_b(part):
                cols = slice(B_CUTS[part], B_CUTS[part + 1])
                lo("bgu", part + 1, bgu[:, 1, cols], bgu_raw[:, cols], bgu[:, 0, cols])

            def lo_wd(i, c, base, rows=P):
                n = 2 * i + c
                at = (n - base) * 2 * H
                lo("wd", n + 1, wd[0:rows, ds(at + H, H)], raw_d[0:rows, c % 2, :], wd[0:rows, ds(at, H)])

            def do_act(i, c, chunk, act, base):
                n = 2 * i + c
                v.wait_ge(s_up, 2 * n + chunk + 1)
                v.wait_ge(s_silu, 2 * n + chunk + 1)
                nc.vector.tensor_tensor(act[:, ds((n - base) * TOK + chunk * CH, CH)], silu[:, chunk, :],
                                        bank[2 * chunk + 1][:, :], ALU.mult).then_inc(s_act, 1)

            def act_pair(q, places, act, count):
                order = ORDER_E if act is act_f else ORDER_B
                for at in places:
                    ft = order[at]
                    rows = CR if act is act_c and ft == SHORT else P
                    lo("act", count + at + 1, pb_t[0:rows, ft, 1, :], act[0:rows, ds(q * PT + ft * TOK, PT)],
                       pb_t[0:rows, ft, 0, :])

            def ad_pair(q):
                v.wait_ge(s_hi["ad"], q + 1)
                for b in range(2):
                    ins = sub(ad_hl[:, :, 1, b, :], ad_raw[:, ds(2 * q + b, 1), :].rearrange(
                        "p o (t r) -> p (o t) r", r=RANK), ad_hl[:, :, 0, b, :])
                ins.then_inc(s_split["ad"], 1)

            nc.vector.memset(v32(pb[:, 0:P]), 0.0).then_inc(s_warm, 1)
            nc.vector.memset(stat[:, :], 0.0).then_inc(s_warm, 1)
            lo_w(0, 0, 0)
            lo_x(0)
            lo_w(0, 0, 1)
            lo_x(1)

            def lo_short(q):
                lo("w", 3 + q, wsh[:, q, :, 1, :, 0:CR], short_raw, wsh[:, q, :, 0, :, 0:CR])
                for b in (2 * q, 2 * q + 1):
                    lo("agu", b + 1, a_part(b, 1), agu_raw[:, b], a_part(b, 0))

            def t_gate_up(chunk):
                for g in range(2):
                    v.wait_ge(s_hi["t"], 2 * chunk + g + 1)
                    for b in range(2):
                        ins = nc.vector.scalar_tensor_tensor(
                            t_rows(chunk, 64, g, b), t_psum(chunk, g, b), own[CR:P, b + 2:b + 3],
                            v32(t_rows(chunk, 0, g, b)), ALU.mult, ALU.subtract)
                ins.then_inc(s_tsplit, 1)

            def short_sums(chunk):
                cols = slice(chunk * CH, chunk * CH + CH)
                for g, ready, done in ((0, s_gate, s_gsum), (1, s_up, s_usum)):
                    v.wait_ge(ready, chunk + 3)
                    nc.vector.tensor_tensor(kept[:, g, cols], kept[:, g, cols], bank[4 + 2 * chunk + g][0:CR, :],
                                            ALU.add).then_inc(done, 1)

            def short_act(chunk):
                v.wait_ge(s_silu, chunk + 3)
                v.wait_ge(s_usum, chunk + 1)
                nc.vector.tensor_tensor(act_c[0:CR, TOK + chunk * CH:TOK + chunk * CH + CH], silu[0:CR, chunk, :],
                                        kept[:, 1, chunk * CH:chunk * CH + CH], ALU.mult).then_inc(s_act, 1)

            for q in range(PAIRS):
                lo_short(q)
            lo_w(0, 2, 0)
            lo_w(0, 2, 1)
            lo_b(0)
            v.wait_ge(s_split["bgu"], 1)
            stack_b(0, 0)
            v.wait_ge(s_const, 6)
            t_gate_up(0)
            stack_b(0, 1)
            for g in range(2):
                ins = nc.vector.tensor_copy(kept[:, g, 0:CH], bank[4 + g][0:CR, :])
            ins.then_inc(s_kept[0], 1)
            do_act(0, 0, 0, act_c, 0)
            t_gate_up(1)
            lo_wd(0, 0, 0)
            lo_wd(0, 1, 0, CR)
            stack_b(0, 2)
            do_act(0, 0, 1, act_c, 0)
            short_sums(0)
            short_sums(1)
            short_act(0)
            short_act(1)

            def tile(i, c, act, base):
                lo_w(i, c + 1, 0)
                lo_w(i, c + 1, 1)
                if base == 0:
                    stack_b(i, c + 1)
                lo_wd(i, c, base)
                do_act(i, c, 0, act, base)
                do_act(i, c, 1, act, base)

            lo_w(0, 3, 0)
            lo_w(0, 3, 1)
            lo_b(1)
            v.wait_ge(s_split["bgu"], 2)
            stack_b(0, 3)
            lo_wd(0, 2, 0)
            do_act(0, 2, 0, act_c, 0)
            do_act(0, 2, 1, act_c, 0)
            lo_b(2)
            v.wait_ge(s_split["bgu"], 3)
            over_tiles(v, 3, FC - 2, lambda i, c: tile(i, c, act_c, 0))
            lo_w(0, FC, 0)
            lo_w(0, FC, 1)
            lo_wd(0, FC - 1, 0)
            do_act(0, FC - 1, 0, act_c, 0)
            ad_pair(0)
            act_pair(0, range(FC), act_c, 0)
            do_act(0, FC - 1, 1, act_c, 0)
            v.wait_ge(s_lnw, 16)

            def norm(q, t):
                m = 2 * q + t
                v.wait_ge(s_ss, m + 1)
                nc.vector.tensor_scalar(stat[:, 1:2], stat[:, 0:1], 1.0 / H, NORM_EPS, ALU.mult, ALU.add
                                        ).then_inc(s_var, 1)
                v.wait_ge(s_std, m + 1)
                nc.vector.reciprocal(stat[:, 3:4], stat[:, 2:3]).then_inc(s_inv, 1)
                v.wait_ge(s_inv, m + 1)
                steps = [
                    lambda: nc.vector.tensor_scalar(stat[:, 4:5], stat[:, 3:4], stat[:, 3:4], stat[:, 1:2],
                                                    ALU.mult, ALU.mult),
                    lambda: nc.vector.tensor_scalar(stat[:, 5:6], stat[:, 4:5], -0.5, 1.5, ALU.mult, ALU.add),
                    lambda: nc.vector.tensor_tensor(stat[:, 6:7], stat[:, 3:4], stat[:, 5:6], ALU.mult),
                ]
                for k, step in enumerate(steps):
                    step().then_inc(s_newton, 1)
                    v.wait_ge(s_newton, 3 * m + k + 1)
                nc.vector.tensor_scalar(tok[:, t, :], Y_BANK[t][:, :], stat[:, 6:7], None, ALU.mult
                                        ).then_inc(s_y_taken, 1)

            def lo_nx(q, t):
                m = 2 * q + t
                raw = silu[:, 1, :].rearrange("p (k n) -> p k n", k=KT)
                v.wait_ge(s_tr, m + 1)
                if t == 1:
                    v.wait_ge(s_split["nx"], m)
                nc.vector.tensor_tensor(raw, TR_BANK[:, :].rearrange("p (k n) -> p k n", k=KT),
                                        lnw[:, :].unsqueeze(2).to_broadcast([P, KT, P]), ALU.mult
                                        ).then_inc(s_nraw, 1)
                lo("nx", m + 1, xT[:, 1, :, ds(m * P, P)], raw, xT[:, 0, :, ds(m * P, P)])

            def pair_b(q, last):
                v.wait_ge(s_tadd, q + 1)
                nc.vector.tensor_tensor(tsum[:, :], T_BANK[0:32, 0:PT], tadd[:, :], ALU.add).then_inc(s_tsum, 1)
                lo("bd", q + 1, wd_t[CR:P, SHORT, 1, :], bd_raw[:, ds(q, 1), :].rearrange("p o h -> p (o h)"),
                   wd_t[CR:P, SHORT, 0, :])
                v.wait_ge(s_hi["t"], q + 5)
                v.wait_ge(s_tsum, q + 1)
                for b in range(2):
                    half = slice(b * P, b * P + P)
                    ins = nc.vector.scalar_tensor_tensor(pb_t[CR:P, SHORT, 1, half], tsum[:, half], own[0:32, b:b + 1],
                                                         v32(pb_t[CR:P, SHORT, 0, half]), ALU.mult, ALU.subtract)
                ins.then_inc(s_tsplit, 1)
                if not last:
                    ad_pair(q + 1)
                    act_pair(q + 1, range(0, 4), act_c, (q + 1) * FC)
                norm(q, 0)
                if not last:
                    act_pair(q + 1, range(4, FC), act_c, (q + 1) * FC)
                norm(q, 1)
                lo_nx(q, 0)
                lo_nx(q, 1)

            with v.Fori(0, PAIRS - 1) as q:
                pair_b(q, False)
            pair_b(PAIRS - 1, True)

            do_act(0, FC, 0, act_f, FC)
            lo_w(0, FC + 1, 0)
            lo_w(0, FC + 1, 1)
            lo_wd(0, FC, FC)
            do_act(0, FC, 1, act_f, FC)
            over_tiles(v, FC + 1, NT - 2, lambda i, c: tile(i, c, act_f, FC))
            lo_wd(0, NT - 1, FC)
            do_act(0, NT - 1, 0, act_f, FC)
            act_pair(0, range(FF), act_f, PAIRS * FC)
            do_act(0, NT - 1, 1, act_f, FC)

            def add_x(q, t):
                v.wait_ge(s_xr_ld[t], 16 * q + 16)
                v.wait_ge(s_y, 2 * q + t + 9)
                nc.vector.tensor_tensor(tok[:, 2 + t, :], tok[:, 2 + t, :], Z_BANK[t][:, :], ALU.add
                                        ).then_inc(s_y_taken, 1)

            with v.Fori(0, PAIRS - 1) as q:
                add_x(q, 0)
                act_pair(q + 1, range(FF), act_f, PAIRS * FC + (q + 1) * FF)
                add_x(q, 1)
            add_x(PAIRS - 1, 0)
            v.wait_ge(s_xr_ld[1], 16 * PAIRS)
            for h, (z, cols) in enumerate(zip(HALF_BANK, HALVES)):
                v.wait_ge(s_y, 4 * PAIRS + h)
                nc.vector.tensor_tensor(tok[:, 3, cols], tok[:, 3, cols], z[:, cols], ALU.add
                                        ).then_inc(s_y_taken, 1)

        @block.tensor
        def _(pe):
            mm = nc.tensor.matmul
            PASSES = ((0, 0), (0, 1), (1, 0))

            def project(par, g, chunk, lora, first=None, cols=(0, CH)):
                lo, hi = cols
                for k in range(KT):
                    if first is not None:
                        pe.wait_ge(s_split["x"], first + k)
                    for s, r in PASSES:
                        last = k == KT - 1 and s == 1 and not lora
                        ins = mm(bank[2 * chunk + g][:, lo:hi], wgu[:, par, g, s, k * P:(k + 1) * P],
                                 xT[:, r, k, chunk * CH + lo:chunk * CH + hi],
                                 start=(k == 0 and s == 0 and r == 0), stop=last)
                return ins

            def lora_gu(par, g, chunk, z, alone):
                for q in (2 * chunk, 2 * chunk + 1):
                    half = (q % 2) * PT
                    ins = mm(z[:, half:half + PT], stack[:, par, q, g * P:(g + 1) * P], tgu(q)[:, g, :],
                             start=(alone and q % 2 == 0), stop=(q % 2 == 1))
                ins.then_inc((s_gate, s_up)[g], 1)

            def short_tile(q, g):
                z = bank[4 + q // 2 * 2 + g]
                for k in range(KT):
                    for s, r in PASSES:
                        ins = mm(z[:, q % 2 * PT:q % 2 * PT + PT], wsh[:, q, g, s, k, :],
                                 xT[:, r, k, q * PT:(q + 1) * PT],
                                 start=(q % 2 == 0 and k == 0 and s == 0 and r == 0),
                                 stop=(q % 2 == 1 and k == KT - 1 and s == 1))
                ins.then_inc(s_t, 1)

            pe.wait_ge(s_warm, 1)
            for _ in range(WARM):
                mm(bank[3][:, :].rearrange("p (k n) -> p k n", k=KT), pb[:, 0:P],
                   pb[:, 0:P].unsqueeze(1).to_broadcast([P, KT, P]), start=True, stop=True)

            pe.wait_ge(s_split["w"], 1)
            project(0, 0, 0, True, first=1)
            pe.wait_ge(s_split["w"], 2)
            project(0, 1, 0, True)
            project(0, 0, 1, True, first=KT + 1)
            project(0, 1, 1, True).then_inc(s_proj0, 1)

            def lora_tile_0(chunk):
                pe.wait_ge(s_tsplit, chunk + 1)
                pe.wait_ge(s_tcopy, chunk + 1)
                for g in range(2):
                    lora_gu(0, g, chunk, bank[2 * chunk + g], False)

            def lora_short():
                pe.wait_ge(s_st_a, 2)
                pe.wait_ge(s_st_v, 2)
                for chunk in range(2):
                    pe.wait_ge(s_kept[chunk], 1)
                    for g in range(2):
                        lora_gu(1, g, chunk, bank[4 + 2 * chunk + g], True)

            for q in range(PAIRS):
                pe.wait_ge(s_split["w"], 3 + q)
                pe.wait_ge(s_split["agu"], 2 * q + 2)
                short_tile(q, 0)
                if q == PAIRS - 1:
                    pe.wait_ge(s_st_a, 1)
                    pe.wait_ge(s_st_v, 1)
                    lora_tile_0(0)
                short_tile(q, 1)
            pe.wait_ge(s_split["w"], 7)
            pe.wait_ge(s_silu, 1)
            project(0, 0, 0, True)
            lora_tile_0(1)
            lora_short()
            pe.wait_ge(s_split["w"], 8)
            pe.wait_ge(s_act, 1)
            project(0, 1, 0, True)
            pe.wait_ge(s_st_a, 3)
            pe.wait_ge(s_st_v, 3)
            for g in range(2):
                lora_gu(0, g, 0, bank[g], False)
            for g in range(2):
                pe.wait_ge((s_silu, s_act)[g], 2)
                project(0, g, 1, True)
                lora_gu(0, g, 1, bank[2 + g], False)

            def tile(i, c, lora):
                n = 2 * i + c
                for chunk in range(2):
                    for g in range(2):
                        if chunk == 0:
                            pe.wait_ge(s_split["w"], 2 * n + g + 3)
                        pe.wait_ge((s_silu, s_act)[g], 2 * n - 2 + chunk + 1)
                        ins = project(c % 2, g, chunk, lora)
                        if lora:
                            if chunk == 0 and g == 0:
                                pe.wait_ge(s_st_a, n + 1)
                                pe.wait_ge(s_st_v, n + 1)
                            lora_gu(c % 2, g, chunk, bank[2 * chunk + g], False)
                        else:
                            ins.then_inc((s_gate, s_up)[g], 1)

            over_tiles(pe, 3, FC - 1, lambda i, c: tile(i, c, True))

            def down(z, ft, t, last, cols=slice(0, H)):
                for s, r in PASSES:
                    ins = mm(z[:, cols], pb_t[:, ft, s, t * P:(t + 1) * P], wd_t[:, ft, r, cols],
                             start=(ft == 0 and s == 0 and r == 0), stop=(ft == last and s == 1))
                return ins

            def transposes(q, t):
                pe.wait_ge(s_y_taken, 2 * q + t + 1)
                if t == 1:
                    pe.wait_ge(s_nraw, 2 * q + 1)
                for k in range(KT):
                    ins = nc.tensor.transpose(TR_BANK[:, k * P:(k + 1) * P], tok[:, t, k * P:(k + 1) * P],
                                              ident[:, :])
                ins.then_inc(s_tr, 1)

            T_AHEAD = 4

            def t_down(q, at):
                ft = ORDER_B[at]
                rows = CR if ft == SHORT else P
                pe.wait_ge(s_split["act"], q * FC + at + 1)
                for r in range(2):
                    ins = mm(T_BANK[:, 0:PT], ad[0:rows, ft, :], pb_t[0:rows, ft, r, :],
                             start=(at == 0 and r == 0), stop=(ft == SHORT and r == 1))
                return ins

            def pair_b(q, first):
                pe.wait_ge(s_split["ad"], q + 1)
                for at in range(T_AHEAD):
                    t_down(q, at)
                if not first:
                    pe.wait_ge(s_y_taken, 2 * q - 1)
                for at, ft in enumerate(ORDER_B[:-1]):
                    if at >= T_AHEAD:
                        t_down(q, at)
                    down(Y_BANK[0], ft, 0, SHORT)
                    if at in (2, 7) and not first:
                        transposes(q - 1, int(at == 7))
                t_down(q, FC - 1).then_inc(s_t, 1)
                for at, ft in enumerate(ORDER_B[:-1]):
                    down(Y_BANK[1], ft, 1, SHORT).then_inc(s_pb_used, 1)
                    if at == 4:
                        pe.wait_ge(s_split["bd"], q + 1)
                        pe.wait_ge(s_tsplit, q + 3)
                        down(Y_BANK[0], SHORT, 0, SHORT).then_inc(s_y, 1)
                down(Y_BANK[1], SHORT, 1, SHORT).then_inc(s_y, 1)

            pe.wait_ge(s_split["wd"], FC)
            pe.wait_ge(s_const, 6)
            pair_b(0, True)
            with pe.Fori(1, PAIRS) as q:
                pair_b(q, False)

            pe.wait_ge(s_split["nx"], 4)
            for g in range(2):
                pe.wait_ge(s_split["w"], 2 * FC + g + 3)
                project(FC % 2, g, 0, False).then_inc((s_gate, s_up)[g], 1)
                transposes(PAIRS - 1, g)
            pe.wait_ge(s_split["nx"], 6)
            for g in range(2):
                project(FC % 2, g, 1, False, cols=(0, PT))
            pe.wait_ge(s_split["nx"], 8)
            for g in range(2):
                project(FC % 2, g, 1, False, cols=(PT, CH)).then_inc((s_gate, s_up)[g], 1)
            over_tiles(pe, FC + 1, NT - 1, lambda i, c: tile(i, c, False))

            pe.wait_ge(s_split["wd"], NT)

            def rows_e(q, t):
                pe.wait_ge(s_y_taken, 2 * q + t + 7)
                for ft in range(FF):
                    if t == 0:
                        pe.wait_ge(s_split["act"], PAIRS * FC + q * FF + ft + 1)
                    ins = down(Z_BANK[t], ft, t, FF - 1)
                    if ft == FF - 1:
                        ins.then_inc(s_y, 1)
                    elif t == 1:
                        ins.then_inc(s_pb_used, 1)

            with pe.Fori(0, PAIRS - 1) as q:
                rows_e(q, 0)
                rows_e(q, 1)
            rows_e(PAIRS - 1, 0)
            for z, cols in zip(HALF_BANK, HALVES):
                for ft in range(FF):
                    ins = down(z, ft, 1, FF - 1, cols)
                ins.then_inc(s_y, 1)


def kernel(**inputs):
    import numpy as np
    import concourse.bacc as bacc
    from concourse.bass_utils import run_bass_kernel_spmd

    def arr(name):
        return np.asarray(inputs[name])

    def pad_rows(w, rows):
        return np.concatenate([w, np.zeros((rows - w.shape[0],) + w.shape[1:], w.dtype)], 0)

    order = list(range(FC - 1))
    order.insert(SHORT, FC - 1)

    def gate_up(gate, up, tiles):
        both = np.stack([pad_rows(gate, tiles * P), pad_rows(up, tiles * P)])
        return both.reshape(2, tiles, P, KT, P).transpose(1, 4, 0, 3, 2).reshape(tiles, P, 2 * H)

    def down(w, tiles):
        return pad_rows(w.T, tiles * P).reshape(tiles, P, H)

    x = arr("x").reshape(TOK, H)
    a_gu = np.stack([arr("L0_cond_A_gate")[0], arr("L0_cond_A_up")[0]])
    b_gu = np.stack([arr("L0_cond_B_gate")[0], arr("L0_cond_B_up")[0]])
    b_gu = np.concatenate([b_gu, np.zeros((2, R, FC * P - b_gu.shape[2], RANK), b_gu.dtype)], 2)
    a_d = arr("L0_cond_A_down")[0]
    a_d = np.concatenate([a_d, np.zeros((R, RANK, FC * P - a_d.shape[2]), a_d.dtype)], 2)
    feeds = {
        "xT_in": x.T.reshape(KT, P, TOK).transpose(1, 0, 2),
        "x_in": x,
        "idx_in": arr("itok_B_2_6").reshape(1, B),
        "wgu_in": np.concatenate([gate_up(arr("L0_cond_W_gate"), arr("L0_cond_W_up"), FC)[order],
                                  gate_up(arr("L0_ffn_gate_w"), arr("L0_ffn_up_w"), FF)], 0),
        "wd_in": np.concatenate([down(arr("L0_cond_W_down"), FC)[order], down(arr("L0_ffn_down_w"), FF)], 0),
        "agu_in": a_gu.reshape(2, R, RANK, KT, P).transpose(1, 4, 0, 3, 2).reshape(R, P, 2 * KT * RANK),
        "bgu_in": b_gu.reshape(2, R, FC, P, RANK)[:, :, order].transpose(1, 4, 2, 0, 3).reshape(R, RANK, 2 * FC * P),
        "ad_in": a_d.reshape(R, RANK, FC, P)[:, :, order].transpose(0, 3, 2, 1).reshape(R, P, FC * RANK),
        "bd_in": arr("L0_cond_B_down")[0].transpose(0, 2, 1),
        "lnw_in": arr("L0_ffn_ln_w").reshape(KT, P).T,
    }
    feeds = {k: np.ascontiguousarray(v) for k, v in feeds.items()}
    nc = bacc.Bacc("TRN2", target_bir_lowering=False, num_devices=1, dynamic_dma_scratch_size=1024)
    args = [nc.dram_tensor(k, v.shape, mybir.dt.from_np(v.dtype), kind="ExternalInput").ap()
            for k, v in feeds.items()]
    out = nc.dram_tensor("out", (TOK, H), mybir.dt.float32, kind="ExternalOutput").ap()
    build(nc, *args, out)
    r = run_bass_kernel_spmd(nc, [feeds], core_ids=[0])
    return r.results[0]["out"].reshape(B, P, H)
```
